# Optimizing a Trainium2 kernel written in Bass

```python
import numpy as np
import jax
import jax.numpy as jnp

def _softmax(x, axis=-1):
    return jax.nn.softmax(x, axis=axis)

def _gelu(x):
    return jax.nn.gelu(x, approximate=True)

def _silu(x):
    return jax.nn.silu(x)

def _sigmoid(x):
    return jax.nn.sigmoid(x)

def _layernorm(x, axis=-1, eps=1e-05):
    m = jnp.mean(x, axis=axis, keepdims=True)
    v = jnp.var(x, axis=axis, keepdims=True)
    return (x - m) / jnp.sqrt(v + eps)

def _scatter_add(tgt, idx, src, axis=0):
    return tgt.at[idx].add(src)

def _segment_sum(src, seg, n):
    return jax.ops.segment_sum(src, seg, n)
kernel_name = 'mk_gnn_resnorm_d4_gnn_r16_f752ca'

def setup_inputs(seed: int=0):
    np.random.seed(seed)
    _w = jnp.asarray

    def _rec_inputs():
        import jax
        import jax.numpy as jnp
        _gk = jax.random.key(seed)
        x = -0.0002117 + 1 * jax.random.normal(jax.random.fold_in(_gk, 1), (6250, 256), jnp.float32)
        src = jax.random.randint(jax.random.fold_in(_gk, 2), (100000,), 0, 6250, jnp.int32)
        dst = jnp.minimum((6250 * jax.random.uniform(jax.random.fold_in(_gk, 3), (100000,)) ** 2.0).astype(jnp.int32), 99999)
        _o = jnp.argsort(dst, stable=True)
        src = src[_o]
        dst = dst[_o]
        edge_weight = jax.random.uniform(jax.random.fold_in(_gk, 13), (100000,), jnp.float32, 0.0, 1)
        return (x, src, dst, edge_weight)
    x, src, dst, edge_weight = _rec_inputs()

    def _L0_gnn_setup():
        import jax, jax.numpy as jnp
        import numpy as np
        N_NODES = 6250
        N_EDGES = 200000
        D_IN = 256
        D_OUT = 256
        key = jax.random.key(seed)
        k1, k2, k3, k4, k5 = jax.random.split(key, 5)
        x = jax.random.normal(k1, (N_NODES, D_IN), dtype=jnp.float32)
        edge_row = jax.random.randint(k2, (N_EDGES,), 0, N_NODES, dtype=jnp.int32)
        edge_col = jax.random.randint(k3, (N_EDGES,), 0, N_NODES, dtype=jnp.int32)
        edge_val = jax.random.uniform(k4, (N_EDGES,), dtype=jnp.float32)
        bound = 1.0 / np.sqrt(D_IN)
        W = jax.random.uniform(k5, (D_OUT, D_IN), dtype=jnp.float32, minval=-bound, maxval=bound)
        return {'x': x, 'edge_row': edge_row, 'edge_col': edge_col, 'edge_val': edge_val, 'W': W}
    _L0_gnn_all = _L0_gnn_setup()
    _L0_gnn_in = {k: v for k, v in _L0_gnn_all.items() if k in ('W',)}
    del _L0_gnn_all

    def _L1_gnn_setup():
        import jax, jax.numpy as jnp
        import numpy as np
        N_NODES = 6250
        BN_EPS = 1e-05

        def gcn_conv(x, src, dst, W, b, n):
            h = x @ W
            loop = jnp.arange(n, dtype=src.dtype)
            s = jnp.concatenate([src, loop])
            d = jnp.concatenate([dst, loop])
            deg = jax.ops.segment_sum(jnp.ones(s.shape, h.dtype), d, num_segments=n)
            dinv = jnp.where(deg > 0, jax.lax.rsqrt(jnp.maximum(deg, 1.0)), 0.0)
            norm = dinv[s] * dinv[d]
            msg = h[s] * norm[:, None]
            out = jax.ops.segment_sum(msg, d, num_segments=n)
            return out + b

        def batch_norm(x, gamma, beta):
            mean = jnp.mean(x, axis=0)
            var = jnp.mean(jnp.square(x - mean), axis=0)
            return (x - mean) * jax.lax.rsqrt(var + BN_EPS) * gamma + beta
        key = jax.random.key(seed)
        ks = jax.random.split(key, 10)
        d0, d1, d2 = (256, 128, 64)
        d_cat = d0 + d1 + d2
        inp = {'node_features': jax.random.normal(ks[0], (N_NODES, d0), jnp.float32), 'edge_idx': jax.random.randint(ks[1], (2, 100000), 0, N_NODES, jnp.int64), 'W1': jax.random.normal(ks[2], (d0, d1), jnp.float32) * (1.0 / np.sqrt(d0)), 'b1': jnp.zeros((d1,), jnp.float32), 'g1': jnp.ones((d1,), jnp.float32), 'be1': jnp.zeros((d1,), jnp.float32), 'W2': jax.random.normal(ks[3], (d1, d2), jnp.float32) * (1.0 / np.sqrt(d1)), 'b2': jnp.zeros((d2,), jnp.float32), 'g2': jnp.ones((d2,), jnp.float32), 'be2': jnp.zeros((d2,), jnp.float32), 'Wfc': jax.random.normal(ks[4], (d_cat, d0), jnp.float32) * (1.0 / np.sqrt(d_cat)), 'bfc': jnp.zeros((d0,), jnp.float32)}
        return inp
    _L1_gnn_all = _L1_gnn_setup()
    _L1_gnn_in = {k: v for k, v in _L1_gnn_all.items() if k in ('W1', 'b1', 'g1', 'be1', 'W2', 'b2', 'g2', 'be2', 'Wfc', 'bfc')}
    del _L1_gnn_all

    def _L2_gnn_setup():
        import jax, jax.numpy as jnp
        import numpy as np
        N = 6250
        D_IN = 256
        D_OUT = 256
        E = 200000
        key = jax.random.key(seed)
        ks = jax.random.split(key, 9)
        x = jax.random.normal(ks[0], (N, D_IN), dtype=jnp.float32)
        edge_src = jax.random.randint(ks[1], (E,), 0, N, dtype=jnp.int32)
        edge_dst = jax.random.randint(ks[2], (E,), 0, N, dtype=jnp.int32)
        edge_weight = jax.random.uniform(ks[3], (E,), dtype=jnp.float32)
        eps = jnp.zeros((1,), dtype=jnp.float32)
        lim1 = 1.0 / np.sqrt(D_IN)
        w1 = jax.random.uniform(ks[4], (D_IN, D_OUT), minval=-lim1, maxval=lim1, dtype=jnp.float32)
        b1 = jax.random.uniform(ks[5], (D_OUT,), minval=-lim1, maxval=lim1, dtype=jnp.float32)
        lim2 = 1.0 / np.sqrt(D_OUT)
        w2 = jax.random.uniform(ks[6], (D_OUT, D_OUT), minval=-lim2, maxval=lim2, dtype=jnp.float32)
        b2 = jax.random.uniform(ks[7], (D_OUT,), minval=-lim2, maxval=lim2, dtype=jnp.float32)
        return {'x': x, 'edge_src': edge_src, 'edge_dst': edge_dst, 'edge_weight': edge_weight, 'eps': eps, 'w1': w1, 'b1': b1, 'w2': w2, 'b2': b2}
    _L2_gnn_all = _L2_gnn_setup()
    _L2_gnn_in = {k: v for k, v in _L2_gnn_all.items() if k in ('eps', 'w1', 'b1', 'w2', 'b2')}
    del _L2_gnn_all

    def _L3_gnn_setup():
        import jax, jax.numpy as jnp
        import numpy as np
        N_NODES = 3125
        N_EDGES = 312500
        WIDTH = 256
        LN_EPS = 1e-05

        def gcn_conv(x, edge_index, W, b):
            n = x.shape[0]
            loops = jnp.arange(n, dtype=edge_index.dtype)
            src = jnp.concatenate([edge_index[0], loops])
            dst = jnp.concatenate([edge_index[1], loops])
            deg = jax.ops.segment_sum(jnp.ones_like(dst, dtype=x.dtype), dst, num_segments=n)
            dinv = jnp.where(deg > 0, jax.lax.rsqrt(deg), 0.0)
            norm = dinv[src] * dinv[dst]
            h = x @ W.T
            msgs = norm[:, None] * h[src]
            out = jax.ops.segment_sum(msgs, dst, num_segments=n)
            return out + b

        def layer_norm(x, gamma, beta):
            mu = jnp.mean(x, axis=-1, keepdims=True)
            var = jnp.mean(jnp.square(x - mu), axis=-1, keepdims=True)
            return (x - mu) * jax.lax.rsqrt(var + LN_EPS) * gamma + beta
        key = jax.random.key(seed)
        k1, k2, k3, k4 = jax.random.split(key, 4)
        x = jax.random.normal(k1, (N_NODES, WIDTH), dtype=jnp.float32)
        edge_index = jax.random.randint(k2, (2, N_EDGES), 0, N_NODES, dtype=jnp.int64)
        W = jax.random.normal(k3, (WIDTH, WIDTH), dtype=jnp.float32) / np.sqrt(WIDTH)
        b = jax.random.normal(k4, (WIDTH,), dtype=jnp.float32) * 0.01
        gamma = jnp.ones((WIDTH,), dtype=jnp.float32)
        beta = jnp.zeros((WIDTH,), dtype=jnp.float32)
        return {'x': x, 'edge_index': edge_index, 'W': W, 'b': b, 'gamma': gamma, 'beta': beta}
    _L3_gnn_all = _L3_gnn_setup()
    _L3_gnn_in = {k: v for k, v in _L3_gnn_all.items() if k in ('W', 'b', 'gamma', 'beta')}
    del _L3_gnn_all
    return {'x': x, 'src': src, 'dst': dst, 'edge_weight': edge_weight, 'L0_gnn_W': _L0_gnn_in['W'], 'L1_gnn_W1': _L1_gnn_in['W1'], 'L1_gnn_b1': _L1_gnn_in['b1'], 'L1_gnn_g1': _L1_gnn_in['g1'], 'L1_gnn_be1': _L1_gnn_in['be1'], 'L1_gnn_W2': _L1_gnn_in['W2'], 'L1_gnn_b2': _L1_gnn_in['b2'], 'L1_gnn_g2': _L1_gnn_in['g2'], 'L1_gnn_be2': _L1_gnn_in['be2'], 'L1_gnn_Wfc': _L1_gnn_in['Wfc'], 'L1_gnn_bfc': _L1_gnn_in['bfc'], 'L2_gnn_eps': _L2_gnn_in['eps'], 'L2_gnn_w1': _L2_gnn_in['w1'], 'L2_gnn_b1': _L2_gnn_in['b1'], 'L2_gnn_w2': _L2_gnn_in['w2'], 'L2_gnn_b2': _L2_gnn_in['b2'], 'L3_gnn_W': _L3_gnn_in['W'], 'L3_gnn_b': _L3_gnn_in['b'], 'L3_gnn_gamma': _L3_gnn_in['gamma'], 'L3_gnn_beta': _L3_gnn_in['beta']}

def reference(x, src, dst, edge_weight, L0_gnn_W, L1_gnn_W1, L1_gnn_b1, L1_gnn_g1, L1_gnn_be1, L1_gnn_W2, L1_gnn_b2, L1_gnn_g2, L1_gnn_be2, L1_gnn_Wfc, L1_gnn_bfc, L2_gnn_eps, L2_gnn_w1, L2_gnn_b1, L2_gnn_w2, L2_gnn_b2, L3_gnn_W, L3_gnn_b, L3_gnn_gamma, L3_gnn_beta):
    import jax
    import jax.numpy as jnp

    def _L0_gnn_ref(x, edge_row, edge_col, edge_val, W):
        import jax, jax.numpy as jnp
        import numpy as np
        N_NODES = 6250
        N_EDGES = 200000
        D_IN = 256
        D_OUT = 256
        msgs = edge_val[:, None] * x[edge_col]
        agg = jax.ops.segment_sum(msgs, edge_row, num_segments=N_NODES)
        return agg @ W.T

    def _L1_gnn_ref(node_features, edge_idx, W1, b1, g1, be1, W2, b2, g2, be2, Wfc, bfc):
        import jax, jax.numpy as jnp
        import numpy as np
        N_NODES = 6250
        BN_EPS = 1e-05

        def gcn_conv(x, src, dst, W, b, n):
            h = x @ W
            loop = jnp.arange(n, dtype=src.dtype)
            s = jnp.concatenate([src, loop])
            d = jnp.concatenate([dst, loop])
            deg = jax.ops.segment_sum(jnp.ones(s.shape, h.dtype), d, num_segments=n)
            dinv = jnp.where(deg > 0, jax.lax.rsqrt(jnp.maximum(deg, 1.0)), 0.0)
            norm = dinv[s] * dinv[d]
            msg = h[s] * norm[:, None]
            out = jax.ops.segment_sum(msg, d, num_segments=n)
            return out + b

        def batch_norm(x, gamma, beta):
            mean = jnp.mean(x, axis=0)
            var = jnp.mean(jnp.square(x - mean), axis=0)
            return (x - mean) * jax.lax.rsqrt(var + BN_EPS) * gamma + beta
        n = node_features.shape[0]
        src, dst = (edge_idx[0], edge_idx[1])
        feats = [node_features]
        x = node_features
        x = gcn_conv(x, src, dst, W1, b1, n)
        x = jax.nn.relu(batch_norm(x, g1, be1))
        feats.append(x)
        x = gcn_conv(x, src, dst, W2, b2, n)
        x = jax.nn.relu(batch_norm(x, g2, be2))
        feats.append(x)
        cat = jnp.concatenate(feats, axis=1)
        return jax.nn.relu(cat @ Wfc + bfc)

    def _L2_gnn_ref(x, edge_src, edge_dst, edge_weight, eps, w1, b1, w2, b2):
        import jax, jax.numpy as jnp
        import numpy as np
        N = 6250
        D_IN = 256
        D_OUT = 256
        E = 200000
        msgs = edge_weight[:, None] * x[edge_src]
        agg = jax.ops.segment_sum(msgs, edge_dst, num_segments=N)
        h = (1.0 + eps[0]) * x + agg
        h = jax.nn.relu(h @ w1 + b1)
        return h @ w2 + b2

    def _L3_gnn_ref(x, edge_index, W, b, gamma, beta):
        import jax, jax.numpy as jnp
        import numpy as np
        N_NODES = 3125
        N_EDGES = 312500
        WIDTH = 256
        LN_EPS = 1e-05

        def gcn_conv(x, edge_index, W, b):
            n = x.shape[0]
            loops = jnp.arange(n, dtype=edge_index.dtype)
            src = jnp.concatenate([edge_index[0], loops])
            dst = jnp.concatenate([edge_index[1], loops])
            deg = jax.ops.segment_sum(jnp.ones_like(dst, dtype=x.dtype), dst, num_segments=n)
            dinv = jnp.where(deg > 0, jax.lax.rsqrt(deg), 0.0)
            norm = dinv[src] * dinv[dst]
            h = x @ W.T
            msgs = norm[:, None] * h[src]
            out = jax.ops.segment_sum(msgs, dst, num_segments=n)
            return out + b

        def layer_norm(x, gamma, beta):
            mu = jnp.mean(x, axis=-1, keepdims=True)
            var = jnp.mean(jnp.square(x - mu), axis=-1, keepdims=True)
            return (x - mu) * jax.lax.rsqrt(var + LN_EPS) * gamma + beta
        h = gcn_conv(x, edge_index, W, b)
        h = layer_norm(h, gamma, beta)
        h = jax.nn.relu(h)
        return h
    edge_index = jnp.stack([src, dst])
    x = _layernorm(x + _L0_gnn_ref(x, src, dst, edge_weight, L0_gnn_W), axis=-1)
    x = _layernorm(x + _L1_gnn_ref(x, edge_index, L1_gnn_W1, L1_gnn_b1, L1_gnn_g1, L1_gnn_be1, L1_gnn_W2, L1_gnn_b2, L1_gnn_g2, L1_gnn_be2, L1_gnn_Wfc, L1_gnn_bfc), axis=-1)
    x = _layernorm(x + _L2_gnn_ref(x, src, dst, edge_weight, L2_gnn_eps, L2_gnn_w1, L2_gnn_b1, L2_gnn_w2, L2_gnn_b2), axis=-1)
    x = _layernorm(x + _L3_gnn_ref(x, edge_index, L3_gnn_W, L3_gnn_b, L3_gnn_gamma, L3_gnn_beta), axis=-1)
    return x

_drawn_inputs = setup_inputs


def setup_inputs(seed=0):
    import zlib

    import numpy as np

    out = dict(_drawn_inputs(seed))
    spreads = {'L1_gnn_b1': (0.0, 0.8),
     'L1_gnn_g1': (1.0, 0.2),
     'L1_gnn_be1': (0.0, 0.1),
     'L1_gnn_b2': (0.0, 0.8),
     'L1_gnn_g2': (1.0, 0.2),
     'L1_gnn_be2': (0.0, 0.329),
     'L1_gnn_bfc': (0.0, 0.1),
     'L3_gnn_gamma': (1.0, 0.2),
     'L3_gnn_beta': (0.0, 0.1)}
    factors = {'L2_gnn_b1': 3.635, 'L3_gnn_b': 4.552}
    for name, (base, spread) in spreads.items():
        noise = np.random.default_rng([zlib.crc32(name.encode()), seed]).standard_normal(out[name].shape)
        drawn = base * np.exp(spread * noise) if base else spread * noise
        out[name] = jnp.asarray(drawn.astype(out[name].dtype))
    for name, factor in factors.items():
        out[name] = (out[name] * factor).astype(out[name].dtype)
    return out
```

```python
import concourse.bass as bass
from concourse import mybir

F32 = mybir.dt.float32
BF16 = mybir.dt.bfloat16
I32 = mybir.dt.int32
ALU = mybir.AluOpType
ACT = mybir.ActivationFunctionType
AX = mybir.AxisListType
ET = mybir.EngineType

N = 6250
E = 100000
D = 256
NT = 49
NC = 782
CG = 4
NG = 196
W = 128
AW = 6400
LAST = 6272
RING = 4
SRING = 3
AR = N + 128
EPS = 1e-5
BT = 7
LOADREGS = 14


def rows(t):
    return min(128, N - 128 * t)


def cols(t):
    return slice(128 * t, 128 * t + rows(t))


def chunks(g):
    return min(CG, NC - CG * g)


class Count:

    def __init__(self, nc, name):
        self.sem = nc.alloc_semaphore(name)
        self.n = 0

    def on(self, instruction, k=1):
        instruction.then_inc(self.sem, k)
        self.n += k
        return self.n

    def by(self, engine, value=None):
        value = self.n if value is None else value
        if value > 0:
            engine.wait_ge(self.sem, value)


def build(nc, a, out):
    v, sc, pe, pool, sp = nc.vector, nc.scalar, nc.tensor, nc.gpsimd, nc.sync

    def sb(name, shape, dt=F32):
        return nc.alloc_sbuf_tensor(name, shape, dt)

    def count(name):
        return Count(nc, name)

    accT = sb("accT", [128, 2, AW])
    xT = sb("xT", [128, 2, N])
    degB = sb("degB", [128, AW])
    G = sb("G", [128, RING, CG, D])
    S = sb("S", [128, SRING, CG, W])
    Su = sb("Su", [128, SRING, CG, W], BF16)
    idx = sb("idx", [128, NC], I32)
    early = xT[:, :, :].rearrange("p h n -> p (h n)")
    part = [early[:, 784 * i:784 * i + 784] for i in range(6)]
    tgt = part[0].bitcast(I32)
    srcf, spare, cnt = (q.rearrange("p (g c) -> p g c", c=CG) for q in part[1:4])
    srch = part[4].bitcast(BF16)[:, 0:784]
    srcl = part[4].bitcast(BF16)[:, 784:1568]
    lower = sb("lower", [128, 128])
    identb = sb("identb", [128, 128], BF16)
    pidx = sb("pidx", [128, 1])
    wgt = sb("wgt", [128, NG * CG])
    dst0 = sb("dst0", [128, NG, CG])
    cur = sb("cur", [128, NG, CG])
    base0 = sb("base0", [1, NG], I32)
    base = sb("base", [1, NG], I32)
    rnd = sb("rnd", [1, 2], I32)
    Z = sb("Z", [128, 2 * BT, D])
    XR = sb("XR", [128, 4, D])
    XS = sb("XS", [128, 4, D])
    stat = sb("stat", [128, 2 * BT, 6])
    mv = sb("mv", [128, 2 * BT, 2])
    rstd = sb("rstd", [128, 2 * BT])
    nmr = sb("nmr", [128, 2 * BT])
    bst = sb("bst", [128, 25, 6])
    bmv = sb("bmv", [128, 2])
    bsc = sb("bsc", [128, 4])
    dnm = sb("dnm", [128, NT])
    iota = sb("iota", [128, W])
    ident = sb("ident", [128, 128])
    ones = sb("ones", [1, 128])
    onesb = sb("onesb", [128, 128], BF16)
    epsc = sb("epsc", [128, 1])
    e1 = sb("e1", [128, 1])
    W0 = sb("W0", [128, 2, D])
    W1 = sb("W1", [128, 2, 128])
    W2 = sb("W2", [128, 64])
    Wf = sb("Wf", [128, 3, D])
    Wf3 = sb("Wf3", [64, D])
    M1 = sb("M1", [128, 2, D])
    M2 = sb("M2", [128, 2, D])
    W3 = sb("W3", [128, 2, D])
    vec1 = sb("vec1", [128, 3])
    vec2 = sb("vec2", [64, 3])
    mb1 = sb("mb1", [128, 2])
    rowb = sb("rowb", [1, 2, D])
    l3 = sb("l3", [128, 3, D])

    PS = [nc.alloc_psum_tensor(f"PS{i}", [128, 512], F32) for i in range(8)]

    X1 = nc.dram_tensor("X1", [N, D], F32, kind="Internal").ap()
    X2 = nc.dram_tensor("X2", [N, D], F32, kind="Internal").ap()
    X3 = nc.dram_tensor("X3", [N, D], F32, kind="Internal").ap()
    T1 = nc.dram_tensor("T1", [N, 128], F32, kind="Internal").ap()
    T2 = nc.dram_tensor("T2", [N, 64], F32, kind="Internal").ap()
    T3 = nc.dram_tensor("T3", [N, D], F32, kind="Internal").ap()
    A = [nc.dram_tensor(f"A{k}", [AR, D], F32, kind="Internal").ap() for k in range(CG)]

    s_edge, s_w = count("s_edge"), count("s_w")
    dsti = S[:, 0:2, :, :].bitcast(I32).rearrange("p a b c -> p (a b c)")[:, 0:NG * CG]
    s_edge.on(sp.dma_start(dsti, a["dst"]), 16)
    s_edge.on(sp.dma_start(idx[:, :], a["src"]), 16)
    s_edge.on(sp.dma_start(wgt[:, :], a["edge_weight"]), 16)
    s_zero = [count(f"s_zero{k}") for k in range(CG)]
    halves = lambda ap: ap.rearrange("(k p) n -> p k n", p=128)
    for dst, src in [
        (W0[:, :, :], halves(a["L0_gnn_W"])), (W1[:, :, :], halves(a["L1_gnn_W1"])), (W2[:, :], a["L1_gnn_W2"]),
        (Wf[:, :, :], halves(a["L1_gnn_Wfc"][0:384, :])), (Wf3[:, :], a["L1_gnn_Wfc"][384:448, :]),
        (M1[:, :, :], halves(a["L2_gnn_w1"])), (M2[:, :, :], halves(a["L2_gnn_w2"])), (W3[:, :, :], halves(a["L3_gnn_W"])),
        (vec1[:, :], a["vec1"]), (vec2[:, :], a["vec2"]), (mb1[:, :], a["L2_gnn_b1"]),
        (rowb[0:1, 0, :], a["L1_gnn_bfc"]), (rowb[0:1, 1, :], a["L2_gnn_b2"]), (e1[:, :], a["L2_gnn_eps"]),
        (l3[:, 0, :], a["L3_gnn_b"]), (l3[:, 1, :], a["L3_gnn_gamma"]), (l3[:, 2, :], a["L3_gnn_beta"]),
    ]:
        s_w.on(sp.dma_start(dst, src), 16)

    s_cst, s_d = count("s_cst"), count("s_d")

    def link(ins):
        s_d.on(ins)
        s_d.by(v)

    iti = S[:, 2, 0, :].bitcast(I32)
    s_io = count("s_io")
    s_io.on(pool.iota(iti, pattern=[[1, W]], base=0, channel_multiplier=0))
    pi32 = S[:, 2, 1, 0:1].bitcast(I32)
    s_io.on(pool.iota(pi32, pattern=[[0, 1]], base=0, channel_multiplier=1))
    s_io.on(pool.memset(accT[:, :, :], 0.0))
    s_io.on(pool.memset(lower[:, :], 1.0))
    s_io.on(pool.memset(ident[:, :], 0.0))
    s_io.by(pool)
    s_cst.on(pool.affine_select(out=ident[:, :], in_=ident[:, :], compare_op=ALU.not_equal, fill=1.0, base=0,
                                pattern=[[-1, 128]], channel_multiplier=1))
    s_cst.on(pool.affine_select(out=lower[:, :], in_=lower[:, :], compare_op=ALU.is_gt, fill=0.0, base=0,
                                pattern=[[-1, 128]], channel_multiplier=1))
    s_cst.by(pool)
    pool.tensor_copy(identb[:, :], ident[:, :])
    pool.memset(ones[:, :], 1.0)
    pool.memset(onesb[:, :], 1.0)
    pool.memset(epsc[:, :], EPS)
    pool.memset(mv[:, :, :], 1.0)
    s_cst.on(pool.memset(degB[:, :], 1.0))
    zeros = accT[:, :, :].rearrange("p h n -> p (h n)")
    s_io.by(sp)
    for k in range(CG):
        s_zero[k].on(sp.dma_start(A[k][0:6272, :].rearrange("(p r) d -> p (r d)", p=128), zeros[:, 0:49 * D]), 16)
        s_zero[k].on(sp.dma_start(A[k][6272:AR, :], zeros[0:AR - 6272, 0:D]), 16)

    s_mn, s_par, s_rnd = count("s_mn"), count("s_par"), count("s_rnd")
    red = Z[:, :, :].rearrange("p a b -> p (a b)")
    mnB, mxB, mnN, mxN = (red[:, 256 * i:256 * i + NG] for i in range(4))
    big = red[:, 1024:1024 + NG * CG].rearrange("p (g c) -> p g c", c=CG)
    s_edge.by(v)
    link(v.tensor_copy(dst0[:, :, :], dsti.rearrange("p (g c) -> p g c", c=CG)))
    link(v.tensor_scalar(big, dst0[:, :, :], 0.0, 1.0e6, ALU.is_lt, ALU.mult))
    link(v.tensor_tensor(big, big, dst0[:, :, :], ALU.add))
    link(v.tensor_reduce(mnN, big, AX.X, ALU.min))
    link(v.tensor_scalar(mnN, mnN, -1.0, None, ALU.mult))
    s_mn.on(v.tensor_reduce(mxN, dst0[:, :, :], AX.X, ALU.max))
    s_mn.by(pool)
    RMAX = bass.bass_isa.ReduceOp.max
    s_par.on(pool.partition_all_reduce(mnB, mnN, 128, RMAX))
    s_par.on(pool.partition_all_reduce(mxB, mxN, 128, RMAX))
    s_par.by(v)
    link(v.tensor_scalar(mnB, mnB, -1.0, None, ALU.mult))
    link(v.tensor_tensor(dst0[:, :, :], dst0[:, :, :], mnB.unsqueeze(2).broadcast_to([128, NG, CG]), ALU.subtract))
    link(v.tensor_scalar(base0[:, :], mnB[0:1, :], float(LAST), None, ALU.min))
    link(v.tensor_tensor(mxN, mxB, mnB, ALU.subtract))
    link(v.tensor_reduce(rnd[:, 0:1], mxN[0:1, :], AX.X, ALU.max))
    link(v.tensor_scalar(rnd[:, 1:2], rnd[:, 0:1], 7, None, ALU.logical_shift_right))
    link(v.tensor_scalar(rnd[:, 0:1], rnd[:, 1:2], 1.0, None, ALU.add))
    s_io.by(v)
    link(v.tensor_copy(iota[:, :], iti))
    link(v.tensor_copy(pidx[:, :], pi32))
    tmpi = red[:, 2048:2048 + NC].bitcast(I32)
    link(v.memset(srcf[:, :, :], 0.0))
    link(v.memset(cnt[:, :, :], 0.0))
    srcv = srcf[:, :, :].rearrange("p g c -> p (g c)")[:, 0:NC]
    link(v.tensor_copy(srcv, idx[:, :]))
    link(v.tensor_scalar(tmpi, idx[:, :], 63, None, ALU.bitwise_and))
    link(v.tensor_copy(srcl[:, 0:NC], tmpi))
    link(v.tensor_tensor(tmpi, idx[:, :], tmpi, ALU.subtract))
    link(v.tensor_copy(srch[:, 0:NC], tmpi))
    link(v.tensor_scalar(pidx[:, :], pidx[:, :], float(N), None, ALU.add))
    s_rnd.on(v.tensor_scalar(spare[:, :, :], srcf[:, :, :], -1.0, pidx[:, 0:1], ALU.mult, ALU.add))

    LOOP = [ET.Pool, ET.PE, ET.DVE]
    LOOP0 = LOOP + [ET.Activation, ET.SP]
    for e in (pool, pe, v, sc, sp):
        s_rnd.by(e)
        s_cst.by(e)
        s_w.by(e)
        s_d.by(e)
    R = nc.values_load(rnd[0:1, 0:1], engines=LOOP0, min_val=1, max_val=1 << 20,
                       skip_runtime_bounds_check_because="worked out from the edges")

    s_g = [nc.alloc_semaphore(f"s_g{i}") for i in range(RING)]
    s_S = nc.alloc_semaphore("s_S")
    s_pe = nc.alloc_semaphore("s_pe")
    s_acc = nc.alloc_semaphore("s_acc")
    s_endp = nc.alloc_semaphore("s_endp")
    s_ende = nc.alloc_semaphore("s_ende")
    s_gop = nc.alloc_semaphore("s_gop")
    s_goe = nc.alloc_semaphore("s_goe")
    s_agg = count("s_agg")

    def aggregate(table, width, acc, weighted):
        H = max(1, width // 128)
        F = min(128, width)
        link(v.tensor_copy(cur[:, :, :], dst0[:, :, :]))
        link(v.tensor_copy(base[:, :], base0[:, :]))
        with nc.Fori(0, R, engines=LOOP):
            for g in range(NG):
                k = chunks(g)
                if g >= RING:
                    pool.wait_ge(s_pe, g - RING + 1)
                for j in range(k):
                    c = CG * g + j
                    pool.indirect_dma_start(G[:, g % RING, j, 0:width], None, table,
                                            bass.IndirectOffsetOnAxis(idx[:, c:c + 1], 0)).then_inc(s_g[g % RING], 16)

                pe.wait_ge(s_S, g + 1)
                if g >= 2:
                    pe.wait_ge(s_acc, g - 1)
                arrived = sum(16 * chunks(q) for q in range(g % RING, g + 1, RING))
                pe.wait_ge(s_g[g % RING], arrived)
                for h in range(H):
                    for j in range(k):
                        last = pe.matmul(PS[g % 2][0:F, W * h:W * h + W], G[:, g % RING, j, F * h:F * h + F],
                                         S[:, g % SRING, j, :], start=j == 0, stop=j == k - 1)
                last.then_inc(s_pe, 1)

            def onehot(g):
                if g >= SRING:
                    v.wait_ge(s_pe, g - SRING + 1)
                for j in range(chunks(g)):
                    c = CG * g + j
                    if weighted:
                        last = v.tensor_scalar(S[:, g % SRING, j, :], iota[:, :], cur[:, g, j:j + 1], wgt[:, c:c + 1],
                                               ALU.is_equal, ALU.mult)
                    else:
                        last = v.tensor_scalar(S[:, g % SRING, j, :], iota[:, :], cur[:, g, j:j + 1], None, ALU.is_equal)
                last.then_inc(s_S, 1)

            onehot(0)
            for g in range(NG):
                if g % LOADREGS == 0:
                    los = nc.values_load_multi_w_load_instructions(
                        base[0:1, g:g + LOADREGS], engines=[ET.DVE], min_val=0, max_val=LAST,
                        skip_runtime_bounds_check_because="held under LAST")[1]
                if g + 1 < NG:
                    onehot(g + 1)
                v.wait_ge(s_pe, g + 1)
                if g:
                    v.wait_ge(s_acc, g)
                lo = los[g % LOADREGS]
                aw = acc(lo)
                got = PS[g % 2][0:F, 0:W * H]
                if H > 1:
                    got = got.rearrange("p (h w) -> p h w", h=H)
                v.tensor_tensor(aw, got, aw, ALU.add).then_inc(s_acc, 1)

            for i in range(RING):
                pool.wait_ge(s_g[i], sum(16 * chunks(q) for q in range(i, NG, RING)))
            pool.sem_inc(s_endp, 1)
            pe.sem_inc(s_ende, 1)
            v.wait_ge(s_acc, NG)
            v.wait_ge(s_endp, 1)
            v.wait_ge(s_ende, 1)
            for s in [s_S, s_pe, s_acc, s_endp, s_ende]:
                v.sem_clear(s)
            v.tensor_scalar(cur[:, :, :], cur[:, :, :], float(W), None, ALU.subtract).then_inc(s_acc, 1)
            v.tensor_scalar(base[:, :], base[:, :], float(W), float(LAST), ALU.add, ALU.min).then_inc(s_acc, 1)
            v.wait_ge(s_acc, 2)
            v.sem_clear(s_acc)
            v.sem_inc(s_gop, 1)
            pool.wait_ge(s_gop, 1)
            pool.sem_clear(s_gop)
            pool.dma_reset(range(s_g[0].num, s_g[0].num + RING))
            for s in s_g:
                pool.sem_clear(s)
            pool.sem_inc(s_goe, 1)
            pe.wait_ge(s_goe, 1)
            pe.sem_clear(s_goe)
        v.sem_inc(s_agg.sem, 1)
        s_agg.n += 1

    wide = lambda lo: accT[:, :, bass.ds(lo, W)]

    s_ld = [count(f"s_ld{i}") for i in range(4)]
    s_st = [count(f"s_st{i}") for i in range(2 * BT)]
    s_st2 = [count(f"s_st2{i}") for i in range(4)]
    s_mm, s_z, s_ag, s_sq, s_rs = count("s_mm"), count("s_z"), count("s_ag"), count("s_sq"), count("s_rs")
    s_nm, s_tp, s_tc, s_xs = count("s_nm"), count("s_tp"), count("s_tc"), count("s_xs")
    s_ve = count("s_ve")
    s_dn = count("s_dn")

    def stats(z, slot, r):
        link(v.bn_stats(stat[0:r, slot, :], z))
        s_ag.on(v.bn_aggr(mv[0:r, slot, :], stat[0:r, slot, :]))

    def scales(b0, n):
        s_ag.by(sc)
        s_sq.on(sc.activation(rstd[:, b0:b0 + n], mv[:, b0:b0 + n, 1], ACT.Sqrt, bias=epsc[:, 0:1]))
        s_sq.by(v)
        link(v.reciprocal(rstd[:, b0:b0 + n], rstd[:, b0:b0 + n]))
        s_rs.on(v.scalar_tensor_tensor(nmr[:, b0:b0 + n], mv[:, b0:b0 + n, 0], -1.0, rstd[:, b0:b0 + n], ALU.mult, ALU.mult))

    def rows_out(products, residual, combine, store, store2, transposed, ready):
        z_done, nm_done, tc_done = {}, {}, {}
        mm_done = {}
        ld_val = {}
        st_val = {}
        mm0 = {}

        def load(t):
            if t >= 4:
                s_z.by(sp, z_done[t - 4])
            ld_val[t] = s_ld[t % 4].on(sp.dma_start(XR[0:rows(t), t % 4, :], residual[cols(t), :]), 16)

        def multiply(t):
            ready(pe, t)
            if t >= 2:
                s_z.by(pe, z_done[t - 2])
            ops = products(t)
            for i, (l, r) in enumerate(ops):
                ins = pe.matmul(PS[4 + t % 2][0:rows(t), 0:D], l, r, start=i == 0, stop=i == len(ops) - 1)
            mm_done[t] = s_mm.on(ins)

        def transpose(t):
            r = rows(t)
            src = XS[0:r, t % 4, :] if store2 is not None else Z[0:r, t % (2 * BT), :]
            (s_xs if store2 is not None else s_nm).by(pe, xs_done[t] if store2 is not None else nm_done[t])
            if t >= 2:
                s_tc.by(pe, tc_done[t - 2])
            for h in range(2):
                ins = pe.transpose(PS[6 + t % 2][0:128, 128 * h:128 * h + r], src[:, 128 * h:128 * h + 128], ident[0:r, 0:r])
            tp = s_tp.on(ins)
            s_tp.by(sc, tp)
            tc_done[t] = transposed(t, PS[6 + t % 2][:, 0:256].rearrange("p (h w) -> p h w", h=2)[:, :, 0:r])

        xs_done = {}
        for t in range(4):
            load(t)
        nb = NT // BT
        for b in range(nb + 1):
            if b < nb:
                b0 = (b % 2) * BT
                for i in range(BT):
                    t = b * BT + i
                    r = rows(t)
                    multiply(t)
                    z = Z[0:r, b0 + i, :]
                    s_ld[t % 4].by(v, ld_val[t])
                    s_mm.by(v, mm_done[t])
                    if t >= 2 * BT and store is not None:
                        s_st[b0 + i].by(v, st_val[t - 2 * BT])
                    if t >= 2 * BT and transposed is not None:
                        s_tp.by(v)
                    z_done[t] = combine(t, z, PS[4 + t % 2][0:r, 0:D], XR[0:r, t % 4, :])
                    if t + 4 < NT:
                        load(t + 4)
                    stats(z, b0 + i, r)
                scales(b0, BT)
                rs = s_rs.n
            if b >= 1:
                p0 = ((b - 1) % 2) * BT
                for i in range(BT):
                    t = (b - 1) * BT + i
                    r = rows(t)
                    s_rs.by(sc, prev_rs)
                    z = Z[0:r, p0 + i, :]
                    nm_done[t] = s_nm.on(sc.activation(z, z, ACT.Identity, scale=rstd[0:r, p0 + i:p0 + i + 1],
                                                       bias=nmr[0:r, p0 + i:p0 + i + 1]))
                    if store2 is not None:
                        if t >= 4:
                            s_st2[t % 4].by(v, st_val[(2, t - 4)])
                            if transposed is not None:
                                s_tp.by(v)
                        s_nm.by(v, nm_done[t])
                        xs_done[t] = s_xs.on(v.tensor_scalar(XS[0:r, t % 4, :], z, dnm[0:r, t:t + 1], None, ALU.mult))
                    if transposed is not None:
                        transpose(t)
                    s_nm.by(sp, nm_done[t])
                    st_val[t] = s_st[p0 + i].on(sp.dma_start(store[cols(t), :], z), 16)
                    if store2 is not None:
                        s_xs.by(sp, xs_done[t])
                        st_val[(2, t)] = s_st2[t % 4].on(sp.dma_start(store2[cols(t), :], XS[0:r, t % 4, :]), 16)
            if b < nb:
                prev_rs = rs

    def stored(engine):
        for s in s_st + s_st2:
            s.by(engine)

    def plain(t, z, p, x):
        return s_zl(v.tensor_tensor(z, p, x, ALU.add))

    def relu_add(t, z, p, x):
        return s_zl(v.scalar_tensor_tensor(z, p, 0.0, x, ALU.max, ALU.add))

    def s_zl(ins):
        n = s_z.on(ins)
        s_z.by(v)
        return n

    def spread():
        link(v.tensor_copy(cur[:, :, :], dst0[:, :, :]))
        link(v.tensor_copy(base[:, :], base0[:, :]))
        s_d.by(sp)
        for k in range(CG):
            s_zero[k].by(pool)
        last2 = lambda g: (chunks(g) + 1) // 2
        pairs = lambda g: 2 * g
        with nc.Fori(0, R, engines=LOOP0):
            def load_x(g):
                if g % LOADREGS == 0:
                    spread.los = nc.values_load_multi_w_load_instructions(
                        base[0:1, g:g + LOADREGS], engines=[ET.SP], min_val=0, max_val=LAST,
                        skip_runtime_bounds_check_because="held under LAST")[1]
                if g >= 4:
                    sp.wait_ge(s_Y, 2 * (g - 3))
                sp.dma_start(XR[:, g % 4, :], a["xpad"][bass.ds(spread.los[g % LOADREGS], 128), :]).then_inc(s_x[g % 4], 16)

            def source_rows(g):
                if g >= 2:
                    pe.wait_ge(s_b, g - 1)
                for j in range(chunks(g)):
                    c = CG * g + j
                    o = PS[g % 2][:, 128 * j:128 * j + 128]
                    pe.matmul(o, srch[:, c:c + 1].broadcast_to([128, 128]), identb[:, :], start=True, stop=False)
                    last = pe.matmul(o, srcl[:, c:c + 1].broadcast_to([128, 128]), identb[:, :], start=False, stop=True)
                last.then_inc(s_sr, 1)

            def prepare(g):
                k = chunks(g)
                if g >= 2:
                    v.wait_ge(s_M, g - 1)
                for j in range(k):
                    c = CG * g + j
                    v.tensor_scalar(Su[:, g % 2, j, :], iota[:, :], cur[:, g, j:j + 1], None, ALU.is_equal)
                    v.tensor_scalar(S[:, g % 2, j, :], iota[:, :], cur[:, g, j:j + 1], wgt[:, c:c + 1],
                                    ALU.is_equal, ALU.mult)
                v.wait_ge(s_sr, g + 1)
                v.tensor_tensor(Eq[:, g % 2, 0:k, :], PS[g % 2][:, 0:128 * k].rearrange("p (j e) -> p j e", j=k),
                                srcf[:, g, 0:k].unsqueeze(2).broadcast_to([128, k, 128]), ALU.is_equal).then_inc(s_eq, 1)
                v.wait_ge(s_eq, g + 1)
                for j in range(k):
                    last = v.tensor_tensor_reduce(out=junk[:, j, :], in0=Eq[:, g % 2, j, :], in1=lower[:, :], scale=1.0, scalar=0.0,
                                                  op0=ALU.mult, op1=ALU.add, accum_out=cnt[:, g, j:j + 1])
                last.then_inc(s_cn, 1)
                v.wait_ge(s_cn, 2 * g + 1)
                v.scalar_tensor_tensor(cnt[:, g, 0:k], cnt[:, g, 0:k], 0.0, spare[:, g, 0:k], ALU.is_gt, ALU.mult).then_inc(s_cn, 1)
                v.wait_ge(s_cn, 2 * g + 2)
                v.tensor_tensor(tgt[:, CG * g:CG * g + k], cnt[:, g, 0:k], srcf[:, g, 0:k], ALU.add).then_inc(s_b, 1)

            def routes(g):
                k = chunks(g)
                pe.wait_ge(s_b, g + 1)
                if g >= 2:
                    pe.wait_ge(s_da, g - 1)
                for j in range(k):
                    pe.matmul(PS[6 + g % 2][:, 0:W], onesb[:, :], Su[:, g % 2, j, :], start=j == 0, stop=j == k - 1)
                if g >= 2:
                    pe.wait_ge(s_mc, g - 1)
                for j in range(k):
                    last = pe.matmul(PS[2 + g % 2][:, 128 * j:128 * j + 128], S[:, g % 2, j, :], Eq[:, g % 2, j, :],
                                     start=True, stop=True)
                last.then_inc(s_M, 1)

            def routes_out(g):
                k = chunks(g)
                sc.wait_ge(s_M, g + 1)
                if g >= 2:
                    sc.wait_ge(s_Y, 2 * (g - 1))
                sc.activation(Ms[:, g % 2, 0:128 * k], PS[2 + g % 2][:, 0:128 * k], ACT.Identity).then_inc(s_mc, 1)

            def messages(g):
                pe.wait_ge(s_mc, g + 1)
                pe.wait_ge(s_x[g % 4], 16 * (g // 4 + 1))
                for q in range(2):
                    n = 2 * g + q
                    if n >= 2:
                        pe.wait_ge(s_yc, n - 1)
                    js = [j for j in (2 * q, 2 * q + 1) if j < chunks(g)]
                    for j in js:
                        last = pe.matmul(PS[4 + n % 2][:, D * (j % 2):D * (j % 2) + D], Ms[:, g % 2, 128 * j:128 * j + 128],
                                         XR[:, g % 4, :], start=True, stop=True)
                    if js:
                        last.then_inc(s_Y, 1)

            def messages_out(g):
                if g >= RING:
                    for j in range(CG):
                        sc.wait_ge(s_k[j], 16 * (g - RING + 1))
                for q in range(2):
                    n = 2 * g + q
                    js = [j for j in (2 * q, 2 * q + 1) if j < chunks(g)]
                    if js:
                        sc.wait_ge(s_Y, n + 1)
                        sc.activation(G[:, g % RING, js[0]:js[-1] + 1, :],
                                      PS[4 + n % 2][:, 0:D * len(js)].rearrange("p (j d) -> p j d", j=len(js)),
                                      ACT.Identity).then_inc(s_yc, 1)

            for g in range(NG):
                load_x(g)
            source_rows(0)
            for g in range(NG + 1):
                if g + 1 < NG:
                    source_rows(g + 1)
                if g < NG:
                    routes(g)
                    routes_out(g)
                if g >= 1:
                    messages(g - 1)
                    messages_out(g - 1)
            for g in range(NG):
                pool.wait_ge(s_b, g + 1)
                for j in range(chunks(g)):
                    c = CG * g + j
                    if j % 2 == 0:
                        pool.wait_ge(s_yc, 2 * g + j // 2 + 1)
                    if g:
                        pool.wait_ge(s_k[j], 16 * g)
                    pool.indirect_dma_start(A[j], bass.IndirectOffsetOnAxis(tgt[:, c:c + 1], 0), G[:, g % RING, j, :], None,
                                            compute_op=ALU.add).then_inc(s_k[j], 16)
            prepare(0)
            for g in range(NG):
                if g % LOADREGS == 0:
                    los = nc.values_load_multi_w_load_instructions(
                        base[0:1, g:g + LOADREGS], engines=[ET.DVE], min_val=0, max_val=LAST,
                        skip_runtime_bounds_check_because="held under LAST")[1]
                if g + 1 < NG:
                    prepare(g + 1)
                v.wait_ge(s_M, g + 1)
                if g:
                    v.wait_ge(s_da, g)
                dw = degB[:, bass.ds(los[g % LOADREGS], W)]
                v.tensor_tensor(dw, PS[6 + g % 2][:, 0:W], dw, ALU.add).then_inc(s_da, 1)

            for j in range(CG):
                pool.wait_ge(s_k[j], 16 * sum(j < chunks(g) for g in range(NG)))
            for e, s in ((pool, s_end[0]), (pe, s_end[1]), (sc, s_end[2]), (sp, s_end[3])):
                e.sem_inc(s, 1)
                v.wait_ge(s, 1)
            v.wait_ge(s_da, NG)
            for s in s_x + s_end + [s_sr, s_b, s_eq, s_cn, s_M, s_mc, s_Y, s_yc, s_da]:
                v.sem_clear(s)
            v.tensor_scalar(cur[:, :, :], cur[:, :, :], float(W), None, ALU.subtract).then_inc(s_da, 1)
            v.tensor_scalar(base[:, :], base[:, :], float(W), float(LAST), ALU.add, ALU.min).then_inc(s_da, 1)
            v.wait_ge(s_da, 2)
            v.sem_clear(s_da)
            for i, e in ((0, pool), (1, pe), (3, sp)):
                v.sem_inc(s_go[i], 1)
                e.wait_ge(s_go[i], 1)
                e.sem_clear(s_go[i])
            pool.dma_reset(range(s_k[0].num, s_k[0].num + CG))
            for s in s_k:
                pool.sem_clear(s)
            pool.sem_inc(s_go[2], 1)
            sc.wait_ge(s_go[2], 1)
            sc.sem_clear(s_go[2])
        v.sem_inc(s_agg.sem, 1)
        s_agg.n += 1
        pool.sem_inc(s_spread.sem, 1)
        s_spread.n += 1

    s_x = [nc.alloc_semaphore(f"s_x{i}") for i in range(4)]
    s_k = [nc.alloc_semaphore(f"s_k{i}") for i in range(CG)]
    s_end = [nc.alloc_semaphore(f"s_end{i}") for i in range(4)]
    s_go = [nc.alloc_semaphore(f"s_go{i}") for i in range(4)]
    s_sr, s_b, s_eq, s_cn, s_M, s_mc, s_Y, s_yc, s_da = (
        nc.alloc_semaphore(n) for n in ("s_sr", "s_b", "s_eq", "s_cn", "s_M", "s_mc", "s_Y", "s_yc", "s_da"))
    s_spread = count("s_spread")
    Eq = Z[:, 0:4, :].rearrange("p a b -> p (a b)").rearrange("p (r j e) -> p r j e", r=2, j=CG)
    Ms = Z[:, 4:8, :].rearrange("p a b -> p (a b)").rearrange("p (r n) -> p r n", r=2)
    junk = Z[:, 8:10, :].rearrange("p a b -> p (a b)").rearrange("p (j e) -> p j e", j=CG)

    spread()

    s_agg.by(sc)
    s_q = count("s_q")
    s_q.on(sc.activation(degB[:, 0:N], degB[:, 0:N], ACT.Sqrt))
    s_q.by(v)
    s_dn.on(v.reciprocal(degB[:, 0:N], degB[:, 0:N]))
    s_agg.by(pe)
    s_dn.by(pe)
    for t in range(NT):
        ins = pe.matmul(PS[2][0:rows(t), t:t + 1], degB[0:1, cols(t)], ones[0:1, 0:1], start=True, stop=True)
    s_dt = count("s_dt")
    s_dt.on(ins)
    s_dt.by(v)
    link(v.memset(dnm[:, :], 0.0))
    v.tensor_copy(dnm[:, 0:NT - 1], PS[2][:, 0:NT - 1])
    link(v.tensor_copy(dnm[0:rows(NT - 1), NT - 1:NT], PS[2][0:rows(NT - 1), NT - 1:NT]))
    s_d.by(sc)

    def to_xT(t, p):
        return s_tc.on(sc.activation(xT[:, :, cols(t)], p, ACT.Identity))

    s_al = [count(f"s_al{i}") for i in range(RING)]
    s_a1, s_a2, s_at, s_ac = count("s_a1"), count("s_a2"), count("s_at"), count("s_ac")
    s_spread.by(sp)
    summed = {}

    def sum_up(t):
        r, slot = rows(t), t % RING
        if t >= RING:
            s_at.by(sp, summed[t - RING][0])
        for k in range(CG):
            n = s_al[slot].on(sp.dma_start(G[0:r, slot, k, :], A[k][cols(t), :]), 16)
        s_al[slot].by(pool, n)
        s_a1.on(pool.tensor_tensor(G[0:r, slot, 0:2, :], G[0:r, slot, 0:2, :], G[0:r, slot, 2:4, :], ALU.add))
        s_a1.by(v)
        s_a2.on(v.tensor_tensor(G[0:r, slot, 0, :], G[0:r, slot, 0, :], G[0:r, slot, 1, :], ALU.add))
        s_a2.by(pe)
        if t >= 2:
            s_ac.by(pe, summed[t - 2][1])
        o = PS[t % 2]
        for h in range(2):
            ins = pe.transpose(o[:, 128 * h:128 * h + r], G[0:r, slot, 0, 128 * h:128 * h + 128], ident[0:r, 0:r])
        n = s_at.on(ins)
        s_at.by(sc, n)
        summed[t] = (n, s_ac.on(sc.activation(accT[:, :, cols(t)],
                                              o[:, 0:256].rearrange("p (h w) -> p h w", h=2)[:, :, 0:r], ACT.Identity)))

    def summed_up(e, t):
        for q in range(4) if t == 0 else [t + 3]:
            if q < NT:
                sum_up(q)
        s_ac.by(e, summed[t][1])

    rows_out(lambda t: [(accT[:, h, cols(t)], W0[:, h, :]) for h in range(2)], a["xpad"], plain, X1, None, to_xT,
             summed_up)

    s_h, s_hs = count("s_h"), count("s_hs")
    s_ht = [count(f"s_ht{i}") for i in range(4)]
    s_hb, s_hc = count("s_hb"), count("s_hc")

    def first_table(table, width, lhs, rhs, init, lhs2, rhs2):
        kk = len(rhs)
        hs, ht = {}, {}
        for t in range(NT):
            r = rows(t)
            if t >= 2:
                s_hs.by(pe, hs[t - 2])
            for i in range(kk):
                ins = pe.matmul(PS[4 + t % 2][0:r, 0:width], lhs(i, t), rhs[i], start=i == 0, stop=i == kk - 1)
            s_h.on(ins)
            s_h.by(sc)
            if t >= 4:
                s_ht[t % 4].by(sc, ht[t - 4])
            hs[t] = s_hs.on(sc.activation(XS[0:r, t % 4, 0:width], PS[4 + t % 2][0:r, 0:width], ACT.Identity,
                                          scale=dnm[0:r, t:t + 1]))
            s_hs.by(sp)
            ht[t] = s_ht[t % 4].on(sp.dma_start(table[cols(t), :], XS[0:r, t % 4, 0:width]), 16)
        hc = {}
        for b in range(13):
            lo, n = 512 * b, min(512, N - 512 * b)
            if b >= 2:
                s_hc.by(pe, hc[b - 2])
            for i in range(kk):
                ins = pe.matmul(PS[6 + b % 2][0:width, 0:n], rhs[i], lhs2(i, lo, n), start=i == 0, stop=i == kk - 1)
            s_hb.on(ins)
            s_hb.by(v)
            hc[b] = s_hc.on(v.tensor_tensor(init[:, lo:lo + n], PS[6 + b % 2][0:width, 0:n], degB[0:width, lo:lo + n], ALU.mult))
        s_hc.by(v)
        for s in s_ht:
            s.by(pool)

    def batch_norm(x, F, vec):
        link(v.tensor_tensor(x, x, degB[0:F, 0:N], ALU.mult))
        link(v.tensor_scalar(x, x, vec[:, 0:1], None, ALU.add))
        for i in range(25):
            s_d.on(v.bn_stats(bst[0:F, i, :], x[:, 250 * i:250 * i + 250]))
        s_d.by(v)
        s_ag.on(v.bn_aggr(bmv[0:F, :], bst[0:F, :, :]))
        s_ag.by(sc)
        s_sq.on(sc.activation(bsc[0:F, 0:1], bmv[0:F, 1:2], ACT.Sqrt, bias=epsc[0:F, 0:1]))
        s_sq.by(v)
        link(v.reciprocal(bsc[0:F, 1:2], bsc[0:F, 0:1]))
        link(v.tensor_tensor(bsc[0:F, 2:3], bsc[0:F, 1:2], vec[:, 1:2], ALU.mult))
        link(v.scalar_tensor_tensor(bsc[0:F, 3:4], bmv[0:F, 0:1], -1.0, bsc[0:F, 2:3], ALU.mult, ALU.mult))
        link(v.tensor_tensor(bsc[0:F, 3:4], bsc[0:F, 3:4], vec[:, 2:3], ALU.add))
        s_d.by(sc)
        s_ve.on(sc.activation(x, x, ACT.Relu, scale=bsc[0:F, 2:3], bias=bsc[0:F, 3:4]))
        s_ve.by(pe)

    s_tc.by(pe)
    x1T = accT[:, 0, 0:N]
    x2T = accT[0:64, 1, 0:N]
    s_mm.by(v)
    first_table(T1, 128, lambda i, t: xT[:, i, cols(t)], [W1[:, 0, :], W1[:, 1, :]], x1T,
                lambda i, lo, n: xT[:, i, lo:lo + n], None)
    aggregate(T1, 128, lambda lo: accT[:, 0, bass.ds(lo, W)], False)
    batch_norm(x1T, 128, vec1)
    first_table(T2, 64, lambda i, t: accT[:, 0, cols(t)], [W2[:, :]], x2T,
                lambda i, lo, n: accT[:, 0, lo:lo + n], None)
    aggregate(T2, 64, lambda lo: accT[0:64, 1, bass.ds(lo, W)], False)
    batch_norm(x2T, 64, vec2)

    s_e = count("s_e")
    s_e.on(v.tensor_scalar(e1[:, :], e1[:, :], 1.0, None, ALU.add))
    s_e.by(sc)

    def cat(t):
        return [(xT[:, 0, cols(t)], Wf[:, 0, :]), (xT[:, 1, cols(t)], Wf[:, 1, :]), (accT[:, 0, cols(t)], Wf[:, 2, :]),
                (accT[0:64, 1, cols(t)], Wf3[:, :]), (ones[0:1, 0:rows(t)], rowb[0:1, 0, :])]

    def to_acc(t, p):
        s_mm.by(sc)
        return s_tc.on(sc.activation(accT[:, :, cols(t)], p, ACT.Identity, scale=e1[:, 0:1]))

    stored(sp)
    rows_out(cat, X1, relu_add, X2, None, to_acc, lambda e, t: None)

    stored(pool)
    s_tc.by(v)
    aggregate(X2, D, wide, True)
    s_u, s_uc = count("s_u"), count("s_uc")
    s_agg.by(pe)
    uc = []
    for b in range(13):
        lo, n = 512 * b, min(512, N - 512 * b)
        for o in range(2):
            i = len(uc)
            if i >= 2:
                s_uc.by(pe, uc[i - 2])
            for h in range(2):
                ins = pe.matmul(PS[6 + i % 2][:, 0:n], M1[:, h, 128 * o:128 * o + 128], accT[:, h, lo:lo + n],
                                start=h == 0, stop=h == 1)
            s_u.on(ins)
            s_u.by(sc)
            uc.append(s_uc.on(sc.activation(xT[:, o, lo:lo + n], PS[6 + i % 2][:, 0:n], ACT.Relu, bias=mb1[:, o:o + 1])))

    def to_acc3(t, p):
        return s_tc.on(sc.activation(accT[:, :, cols(t)], p, ACT.Identity))

    rows_out(lambda t: [(xT[:, h, cols(t)], M2[:, h, :]) for h in range(2)] + [(ones[0:1, 0:rows(t)], rowb[0:1, 1, :])],
             X2, plain, X3, T3, to_acc3, lambda e, t: s_uc.by(e, uc[2 * (t // 4) + 1]))

    stored(pool)
    s_tc.by(v)
    aggregate(T3, D, wide, False)
    s_agg.by(pe)
    s_l = count("s_l")

    def last_layer(t, z, p, x):
        r = rows(t)
        m = (t % 2) * BT + 0
        z0 = s_zz(v.scalar_tensor_tensor(z, p, dnm[0:r, t:t + 1], l3[0:r, 0, :], ALU.mult, ALU.add))
        slot = t % 4
        link(v.bn_stats(bst[0:r, slot, :], z))
        s_l.on(v.bn_aggr(bst[0:r, 4 + slot, 0:2], bst[0:r, slot, :]))
        s_l.by(sc)
        q = s_sq.on(sc.activation(bst[0:r, 8 + slot, 0:1], bst[0:r, 4 + slot, 1:2], ACT.Sqrt, bias=epsc[0:r, 0:1]))
        s_sq.by(v, q)
        link(v.reciprocal(bst[0:r, 12 + slot, 0:1], bst[0:r, 8 + slot, 0:1]))
        link(v.tensor_scalar(z, z, bst[0:r, 4 + slot, 0:1], bst[0:r, 12 + slot, 0:1], ALU.subtract, ALU.mult))
        link(v.tensor_tensor(z, z, l3[0:r, 1, :], ALU.mult))
        link(v.tensor_tensor(z, z, l3[0:r, 2, :], ALU.add))
        return s_zl(v.scalar_tensor_tensor(z, z, 0.0, x, ALU.max, ALU.add))

    def s_zz(ins):
        link(ins)

    stored(sp)
    rows_out(lambda t: [(accT[:, h, cols(t)], W3[:, h, :]) for h in range(2)], X3, last_layer, out, None, None,
             lambda e, t: None)
    stored(sp)


_GIVEN = ["xpad", "src", "dst", "edge_weight", "L0_gnn_W", "L1_gnn_W1", "L1_gnn_W2", "L1_gnn_Wfc", "L1_gnn_bfc", "L2_gnn_eps",
          "L2_gnn_w1", "L2_gnn_b1", "L2_gnn_w2", "L2_gnn_b2", "L3_gnn_W", "L3_gnn_b", "L3_gnn_gamma", "L3_gnn_beta",
          "vec1", "vec2"]


def kernel(**inputs):
    import numpy as np
    import concourse.bacc as bacc
    from concourse.bass_utils import run_bass_kernel_spmd

    given = {k: np.asarray(v) for k, v in inputs.items()}

    def by_chunk(x, n, fill):
        full = np.full(128 * n, fill, x.dtype)
        full[:E] = x
        return full.reshape(n, 128).T

    given["src"] = by_chunk(given["src"], NC, 0)
    given["dst"] = by_chunk(given["dst"], NG * CG, -1)
    given["edge_weight"] = by_chunk(given["edge_weight"], NG * CG, 0)
    given["L0_gnn_W"] = given["L0_gnn_W"].T
    given["xpad"] = np.concatenate([given["x"], np.zeros((AW - N, D), given["x"].dtype)])
    given["L3_gnn_W"] = given["L3_gnn_W"].T
    for k in ("L3_gnn_b", "L3_gnn_gamma", "L3_gnn_beta"):
        given[k] = np.broadcast_to(given[k], (128, D))
    for k in ("L1_gnn_bfc", "L2_gnn_b2"):
        given[k] = given[k].reshape(1, D)
    given["L2_gnn_eps"] = np.broadcast_to(given["L2_gnn_eps"].reshape(1, 1), (128, 1))
    given["L2_gnn_b1"] = given["L2_gnn_b1"].reshape(2, 128).T
    given["vec1"] = np.stack([given["L1_gnn_b1"], given["L1_gnn_g1"], given["L1_gnn_be1"]], axis=1)
    given["vec2"] = np.stack([given["L1_gnn_b2"], given["L1_gnn_g2"], given["L1_gnn_be2"]], axis=1)

    nc = bacc.Bacc("TRN2", target_bir_lowering=False, num_devices=1)
    arrays, args = {}, {}
    for name in _GIVEN:
        x = np.ascontiguousarray(given[name])
        arrays[f"in_{name}"] = x
        args[name] = nc.dram_tensor(f"in_{name}", x.shape, mybir.dt.from_np(x.dtype), kind="ExternalInput").ap()
    out = nc.dram_tensor("out_y", (N, D), F32, kind="ExternalOutput").ap()
    build(nc, args, out)
    r = run_bass_kernel_spmd(nc, [arrays], core_ids=[0])
    return r.results[0]["out_y"]
```

```python
import concourse.bass as bass
from concourse import mybir

F32 = mybir.dt.float32
BF16 = mybir.dt.bfloat16
I32 = mybir.dt.int32
ALU = mybir.AluOpType
ACT = mybir.ActivationFunctionType
AX = mybir.AxisListType
ET = mybir.EngineType

N = 6250
E = 100000
D = 256
NT = 49
NC = 782
CG = 4
NG = 196
W = 128
AW = 6400
LAST = 6272
RING = 4
EARLY = 6
SRING = 3
AR = N + 128
EPS = 1e-5
ZR0 = 14
ZR = ZR0 + RING * CG
LOADREGS = 14


def rows(t):
    return min(128, N - 128 * t)


def cols(t):
    return slice(128 * t, 128 * t + rows(t))


def chunks(g):
    return min(CG, NC - CG * g)


def copy_of(c):
    return c % 2 if c < EARLY * CG else c % CG


def taken(k, g):
    return sum(copy_of(c) == k for c in range(min(NC, CG * g + CG)))


class Count:

    def __init__(self, nc, name):
        self.sem = nc.alloc_semaphore(name)
        self.n = 0
        self.at = {}

    def on(self, instruction, k=1):
        instruction.then_inc(self.sem, k)
        self.n += k
        return self.n

    def mark(self, t, instruction, k=1):
        self.at[t] = self.on(instruction, k)

    def of(self, engine, t):
        self.by(engine, self.at[t])

    def by(self, engine, value=None):
        value = self.n if value is None else value
        if value > 0:
            engine.wait_ge(self.sem, value)


def build(nc, a, out):
    v, sc, pe, pool, sp = nc.vector, nc.scalar, nc.tensor, nc.gpsimd, nc.sync

    def sb(name, shape, dt=F32):
        return nc.alloc_sbuf_tensor(name, shape, dt)

    def count(name):
        return Count(nc, name)

    accT = sb("accT", [128, 2, AW])
    xT = sb("xT", [128, 2, N])
    degB = sb("degB", [128, AW])
    rows_buf = sb("rows_buf", [128, ZR, D])
    Z = rows_buf[:, 0:ZR0, :]
    G = rows_buf[:, ZR0:ZR, :].rearrange("p (r c) d -> p r c d", c=CG)
    S = sb("S", [128, SRING, CG, W])
    idx = sb("idx", [128, NC], I32)
    early = xT[:, :, :].rearrange("p h n -> p (h n)")
    part = [early[:, 784 * i:784 * i + 784] for i in range(6)]
    tgt = part[0].bitcast(I32)
    srcf, spare, cnt = (q.rearrange("p (g c) -> p g c", c=CG) for q in part[1:4])
    srcA = part[5].rearrange("p (g c) -> p g c", c=CG)
    srch = part[4].bitcast(BF16)[:, 0:784]
    Su = early[:, 4800:5312].bitcast(BF16).rearrange("p (r j w) -> p r j w", r=2, j=CG)
    lower = early[:, 5376:5504]
    identb = early[:, 5504:5568].bitcast(BF16)
    srcl = part[4].bitcast(BF16)[:, 784:1568]
    pidx = sb("pidx", [128, 1])
    wgt = sb("wgt", [128, NG * CG])
    dst0 = sb("dst0", [128, NG, CG])
    cur = sb("cur", [128, NG, CG])
    base0 = sb("base0", [1, NG], I32)
    base = sb("base", [1, NG], I32)
    rnd = sb("rnd", [1, 2], I32)
    XR = sb("XR", [128, 4, D])
    XS = sb("XS", [128, 4, D])
    stat = [sb(f"stat{i}", [128, ZR, 6]) for i in range(2)]
    mv = [sb(f"mv{i}", [128, ZR, 2]) for i in range(2)]
    rstd = [sb(f"rstd{i}", [128, ZR]) for i in range(2)]
    nmr = [sb(f"nmr{i}", [128, ZR]) for i in range(2)]
    bst = sb("bst", [128, 25, 6])
    bmv = sb("bmv", [128, 2])
    bsc = sb("bsc", [128, 4])
    dnm = sb("dnm", [128, NT])
    iota = sb("iota", [128, W])
    ident = sb("ident", [128, 128])
    ones = sb("ones", [1, 128])
    onesb = sb("onesb", [128, 128], BF16)
    epsc = sb("epsc", [128, 1])
    e1 = sb("e1", [128, 1])
    W0 = sb("W0", [128, 2, D])
    W1 = sb("W1", [128, 2, 128])
    W2 = sb("W2", [128, 64])
    Wf = sb("Wf", [128, 3, D])
    Wf3 = sb("Wf3", [64, D])
    M1 = sb("M1", [128, 2, D])
    M2 = sb("M2", [128, 2, D])
    W3 = sb("W3", [128, 2, D])
    vec1 = sb("vec1", [128, 3])
    vec2 = sb("vec2", [64, 3])
    mb1 = sb("mb1", [128, 2])
    rowb = sb("rowb", [128, 2, D])
    l3 = sb("l3", [128, 3, D])

    PS = [nc.alloc_psum_tensor(f"PS{i}", [128, 512], F32) for i in range(8)]

    X1 = nc.dram_tensor("X1", [N, D], F32, kind="Internal").ap()
    X2 = nc.dram_tensor("X2", [N, D], F32, kind="Internal").ap()
    X3 = nc.dram_tensor("X3", [N, D], F32, kind="Internal").ap()
    T1 = nc.dram_tensor("T1", [N, 128], F32, kind="Internal").ap()
    T2 = nc.dram_tensor("T2", [N, 64], F32, kind="Internal").ap()
    T3 = nc.dram_tensor("T3", [N, D], F32, kind="Internal").ap()
    A = nc.dram_tensor("A", [CG * AR, D], F32, kind="Internal").ap()

    s_edge, s_w = count("s_edge"), count("s_w")
    dsti = S[:, 0:2, :, :].bitcast(I32).rearrange("p a b c -> p (a b c)")[:, 0:NG * CG]
    s_edge.on(sp.dma_start(dsti, a["dst"]), 16)
    s_edge.on(sp.dma_start(idx[:, :], a["src"]), 16)
    s_edge.on(sp.dma_start(wgt[:, :], a["edge_weight"]), 16)
    s_zero = [count(f"s_zero{k}") for k in range(CG)]
    halves = lambda ap: ap.rearrange("(k p) n -> p k n", p=128)
    for dst, src in [
        (W0[:, :, :], halves(a["L0_gnn_W"])), (W1[:, :, :], halves(a["L1_gnn_W1"])), (W2[:, :], a["L1_gnn_W2"]),
        (Wf[:, :, :], halves(a["L1_gnn_Wfc"][0:384, :])), (Wf3[:, :], a["L1_gnn_Wfc"][384:448, :]),
        (M1[:, :, :], halves(a["L2_gnn_w1"])), (M2[:, :, :], halves(a["L2_gnn_w2"])), (W3[:, :, :], halves(a["L3_gnn_W"])),
        (vec1[:, :], a["vec1"]), (vec2[:, :], a["vec2"]), (mb1[:, :], a["L2_gnn_b1"]),
        (rowb[:, 0, :], a["L1_gnn_bfc"]), (rowb[:, 1, :], a["L2_gnn_b2"]), (e1[:, :], a["L2_gnn_eps"]),
        (l3[:, 0, :], a["L3_gnn_b"]), (l3[:, 1, :], a["L3_gnn_gamma"]), (l3[:, 2, :], a["L3_gnn_beta"]),
    ]:
        s_w.on(sp.dma_start(dst, src), 16)

    s_cst, s_d = count("s_cst"), count("s_d")

    def link(ins):
        s_d.on(ins)
        s_d.by(v)

    iti = S[:, 2, 0, :].bitcast(I32)
    s_io = count("s_io")
    s_io.on(pool.iota(iti, pattern=[[1, W]], base=0, channel_multiplier=0))
    pi32 = S[:, 2, 1, 0:1].bitcast(I32)
    s_io.on(pool.iota(pi32, pattern=[[0, 1]], base=0, channel_multiplier=1))
    s_io.on(pool.memset(accT[:, :, :], 0.0))
    s_io.on(pool.memset(lower[:, :], 1.0))
    s_io.on(pool.memset(ident[:, :], 0.0))
    s_io.by(pool)
    s_cst.on(pool.affine_select(out=ident[:, :], in_=ident[:, :], compare_op=ALU.not_equal, fill=1.0, base=0,
                                pattern=[[-1, 128]], channel_multiplier=1))
    s_cst.on(pool.affine_select(out=lower[:, :], in_=lower[:, :], compare_op=ALU.is_gt, fill=0.0, base=0,
                                pattern=[[-1, 128]], channel_multiplier=1))
    s_cst.by(pool)
    pool.tensor_copy(identb[:, :], ident[:, :])
    pool.memset(ones[:, :], 1.0)
    pool.memset(onesb[:, :], 1.0)
    pool.memset(epsc[:, :], EPS)
    s_cst.on(pool.memset(degB[:, :], 1.0))
    zeros = accT[:, :, :].rearrange("p h n -> p (h n)")
    s_io.by(sp)
    for k in range(CG):
        s_zero[k].on(sp.dma_start(A[AR * k:AR * k + 6272, :].rearrange("(p r) d -> p (r d)", p=128), zeros[:, 0:49 * D]), 16)
        s_zero[k].on(sp.dma_start(A[AR * k + 6272:AR * k + AR, :], zeros[0:AR - 6272, 0:D]), 16)

    s_mn, s_par, s_rnd = count("s_mn"), count("s_par"), count("s_rnd")
    red = Z.rearrange("p a b -> p (a b)")
    mnB, mxB, mnN, mxN = (red[:, 256 * i:256 * i + NG] for i in range(4))
    big = red[:, 1024:1024 + NG * CG].rearrange("p (g c) -> p g c", c=CG)
    s_edge.by(v)
    link(v.tensor_copy(dst0[:, :, :], dsti.rearrange("p (g c) -> p g c", c=CG)))
    link(v.tensor_scalar(big, dst0[:, :, :], 0.0, 1.0e6, ALU.is_lt, ALU.mult))
    link(v.tensor_tensor(big, big, dst0[:, :, :], ALU.add))
    link(v.tensor_reduce(mnN, big, AX.X, ALU.min))
    link(v.tensor_scalar(mnN, mnN, -1.0, None, ALU.mult))
    s_mn.on(v.tensor_reduce(mxN, dst0[:, :, :], AX.X, ALU.max))
    s_mn.by(pool)
    RMAX = bass.bass_isa.ReduceOp.max
    s_par.on(pool.partition_all_reduce(mnB, mnN, 128, RMAX))
    s_par.on(pool.partition_all_reduce(mxB, mxN, 128, RMAX))
    s_par.by(v)
    link(v.tensor_scalar(mnB, mnB, -1.0, None, ALU.mult))
    link(v.tensor_tensor(dst0[:, :, :], dst0[:, :, :], mnB.unsqueeze(2).broadcast_to([128, NG, CG]), ALU.subtract))
    link(v.tensor_scalar(base0[:, :], mnB[0:1, :], float(LAST), None, ALU.min))
    link(v.tensor_tensor(mxN, mxB, mnB, ALU.subtract))
    link(v.tensor_reduce(rnd[:, 0:1], mxN[0:1, :], AX.X, ALU.max))
    link(v.tensor_scalar(rnd[:, 1:2], rnd[:, 0:1], 7, None, ALU.logical_shift_right))
    link(v.tensor_scalar(rnd[:, 0:1], rnd[:, 1:2], 1.0, None, ALU.add))
    s_io.by(v)
    link(v.tensor_copy(iota[:, :], iti))
    link(v.tensor_copy(pidx[:, :], pi32))
    tmpi = red[:, 2048:2048 + NC].bitcast(I32)
    link(v.memset(srcf[:, :, :], 0.0))
    link(v.memset(cnt[:, :, :], 0.0))
    srcv = srcf[:, :, :].rearrange("p g c -> p (g c)")[:, 0:NC]
    link(v.tensor_copy(srcv, idx[:, :]))
    link(v.tensor_scalar(tmpi, idx[:, :], 63, None, ALU.bitwise_and))
    link(v.tensor_copy(srcl[:, 0:NC], tmpi))
    link(v.tensor_tensor(tmpi, idx[:, :], tmpi, ALU.subtract))
    link(v.tensor_copy(srch[:, 0:NC], tmpi))
    link(v.tensor_scalar(pidx[:, :], pidx[:, :], float(N), None, ALU.add))
    link(v.tensor_copy(srcA[:, :, :], srcf[:, :, :]))
    for c in range(NG * CG):
        if copy_of(c) and (c < EARLY * CG):
            v.tensor_scalar(srcA[:, c // CG, c % CG:c % CG + 1], srcf[:, c // CG, c % CG:c % CG + 1], float(AR * copy_of(c)), None, ALU.add)
    for j in range(1, CG):
        v.tensor_scalar(srcA[:, EARLY:NG, j:j + 1], srcf[:, EARLY:NG, j:j + 1], float(AR * j), None, ALU.add)
    s_rnd.on(v.tensor_scalar(spare[:, :, :], srcf[:, :, :], -1.0, pidx[:, 0:1], ALU.mult, ALU.add))

    LOOP = [ET.Pool, ET.PE, ET.DVE]
    LOOP0 = LOOP + [ET.Activation, ET.SP]
    for e in (pool, pe, v, sc, sp):
        s_rnd.by(e)
        s_cst.by(e)
        s_w.by(e)
        s_d.by(e)
    R = nc.values_load(rnd[0:1, 0:1], engines=LOOP0, min_val=1, max_val=1 << 20,
                       skip_runtime_bounds_check_because="worked out from the edges")

    s_g = [nc.alloc_semaphore(f"s_g{i}") for i in range(RING)]
    s_S = nc.alloc_semaphore("s_S")
    s_pe = nc.alloc_semaphore("s_pe")
    s_acc = nc.alloc_semaphore("s_acc")
    s_endp = nc.alloc_semaphore("s_endp")
    s_ende = nc.alloc_semaphore("s_ende")
    s_gop = nc.alloc_semaphore("s_gop")
    s_goe = nc.alloc_semaphore("s_goe")
    s_agg = count("s_agg")

    def aggregate(table, width, acc, weighted):
        H = max(1, width // 128)
        F = min(128, width)
        link(v.tensor_copy(cur[:, :, :], dst0[:, :, :]))
        link(v.tensor_copy(base[:, :], base0[:, :]))
        with nc.Fori(0, R, engines=LOOP):
            for g in range(NG):
                k = chunks(g)
                if g >= RING:
                    pool.wait_ge(s_pe, g - RING + 1)
                for j in range(k):
                    c = CG * g + j
                    pool.indirect_dma_start(G[:, g % RING, j, 0:width], None, table,
                                            bass.IndirectOffsetOnAxis(idx[:, c:c + 1], 0)).then_inc(s_g[g % RING], 16)

                pe.wait_ge(s_S, g + 1)
                if g >= 2:
                    pe.wait_ge(s_acc, g - 1)
                arrived = sum(16 * chunks(q) for q in range(g % RING, g + 1, RING))
                pe.wait_ge(s_g[g % RING], arrived)
                for h in range(H):
                    for j in range(k):
                        last = pe.matmul(PS[g % 2][0:F, W * h:W * h + W], G[:, g % RING, j, F * h:F * h + F],
                                         S[:, g % SRING, j, :], start=j == 0, stop=j == k - 1)
                last.then_inc(s_pe, 1)

            def onehot(g):
                if g >= SRING:
                    v.wait_ge(s_pe, g - SRING + 1)
                for j in range(chunks(g)):
                    c = CG * g + j
                    if weighted:
                        last = v.tensor_scalar(S[:, g % SRING, j, :], iota[:, :], cur[:, g, j:j + 1], wgt[:, c:c + 1],
                                               ALU.is_equal, ALU.mult)
                    else:
                        last = v.tensor_scalar(S[:, g % SRING, j, :], iota[:, :], cur[:, g, j:j + 1], None, ALU.is_equal)
                last.then_inc(s_S, 1)

            onehot(0)
            for g in range(NG):
                if g % LOADREGS == 0:
                    los = nc.values_load_multi_w_load_instructions(
                        base[0:1, g:g + LOADREGS], engines=[ET.DVE], min_val=0, max_val=LAST,
                        skip_runtime_bounds_check_because="held under LAST")[1]
                if g + 1 < NG:
                    onehot(g + 1)
                v.wait_ge(s_pe, g + 1)
                if g:
                    v.wait_ge(s_acc, g)
                lo = los[g % LOADREGS]
                aw = acc(lo)
                got = PS[g % 2][0:F, 0:W * H]
                if H > 1:
                    got = got.rearrange("p (h w) -> p h w", h=H)
                v.tensor_tensor(aw, got, aw, ALU.add).then_inc(s_acc, 1)

            for i in range(RING):
                pool.wait_ge(s_g[i], sum(16 * chunks(q) for q in range(i, NG, RING)))
            pool.sem_inc(s_endp, 1)
            pe.sem_inc(s_ende, 1)
            v.wait_ge(s_acc, NG)
            v.wait_ge(s_endp, 1)
            v.wait_ge(s_ende, 1)
            for s in [s_S, s_pe, s_acc, s_endp, s_ende]:
                v.sem_clear(s)
            v.tensor_scalar(cur[:, :, :], cur[:, :, :], float(W), None, ALU.subtract).then_inc(s_acc, 1)
            v.tensor_scalar(base[:, :], base[:, :], float(W), float(LAST), ALU.add, ALU.min).then_inc(s_acc, 1)
            v.wait_ge(s_acc, 2)
            v.sem_clear(s_acc)
            v.sem_inc(s_gop, 1)
            pool.wait_ge(s_gop, 1)
            pool.sem_clear(s_gop)
            pool.dma_reset(range(s_g[0].num, s_g[0].num + RING))
            for s in s_g:
                pool.sem_clear(s)
            pool.sem_inc(s_goe, 1)
            pe.wait_ge(s_goe, 1)
            pe.sem_clear(s_goe)
        v.sem_inc(s_agg.sem, 1)
        s_agg.n += 1

    wide = lambda lo: accT[:, :, bass.ds(lo, W)]

    def names(*ns):
        return [count("s_" + n) for n in ns]

    s_ld = [count(f"s_ld{i}") for i in range(4)]
    s_st = [count(f"s_st{i}") for i in range(ZR)]
    s_ts = [count(f"s_ts{i}") for i in range(4)]
    s_al = [count(f"s_al{i}") for i in range(RING)]
    s_mm, s_z, s_nm, s_tp, s_tc, s_xs = names("mm", "z", "nm", "tp", "tc", "xs")
    s_bs, s_ag, s_sq, s_rc, s_nr = ([count(f"s_{n}{i}") for i in range(2)] for n in ("bs", "ag", "sq", "rc", "nr"))
    s_a1, s_a2, s_ta, s_ca, s_h, s_hs, s_hb, s_hc, s_dt, s_q, s_pb = names(
        "a1", "a2", "ta", "ca", "h", "hs", "hb", "hc", "dt", "q", "pb")
    s_bm, s_bb, s_bq, s_ba, s_rl, s_u, s_uc, s_e, s_n1, s_ga, s_be = names(
        "bm", "bb", "bq", "ba", "rl", "u", "uc", "e", "n1", "ga", "be")

    def pipeline(stages):
        stages = sorted(stages, key=lambda x: -x[0])
        for step in range(NT + stages[0][0]):
            for lag, f in stages:
                if 0 <= step - lag < NT:
                    f(step - lag)

    def zs(ring, t):
        return rows_buf[0:rows(t), t % ring, :]

    def residual(src):
        def load(t):
            if t >= 4:
                s_z.of(sp, t - 4)
            s_ld[t % 4].mark(t, sp.dma_start(XR[0:rows(t), t % 4, :], src[cols(t), :]), 16)
        return load

    def multiply(products, ready):
        def f(t):
            ready(t)
            if t >= 2:
                s_z.of(pe, t - 2)
            ops = products(t)
            for i, (l, r) in enumerate(ops):
                ins = pe.matmul(PS[2 + t % 2][0:rows(t), 0:D], l, r, start=i == 0, stop=i == len(ops) - 1)
            s_mm.mark(t, ins)
        return f

    def normalise(lag, ring, w, given, done):
        def bn(t):
            given.of(v, t)
            s_bs[w].mark(t, v.bn_stats(stat[w][0:rows(t), t % ring, :], zs(ring, t)))

        def ag(t):
            s_bs[w].of(v, t)
            s_ag[w].mark(t, v.bn_aggr(mv[w][0:rows(t), t % ring, :], stat[w][0:rows(t), t % ring, :]))

        def root(t):
            k, r = t % ring, rows(t)
            s_ag[w].of(sc, t)
            s_sq[w].mark(t, sc.activation(rstd[w][0:r, k:k + 1], mv[w][0:r, k, 1:2], ACT.Sqrt, bias=epsc[0:r, 0:1]))

        def rec(t):
            k, r = t % ring, rows(t)
            s_sq[w].of(v, t)
            s_rc[w].mark(t, v.reciprocal(rstd[w][0:r, k:k + 1], rstd[w][0:r, k:k + 1]))

        def neg(t):
            k, r = t % ring, rows(t)
            s_rc[w].of(v, t)
            s_nr[w].mark(t, v.scalar_tensor_tensor(nmr[w][0:r, k:k + 1], mv[w][0:r, k, 0:1], -1.0, rstd[w][0:r, k:k + 1],
                                                   ALU.mult, ALU.mult))

        def norm(t):
            k, r = t % ring, rows(t)
            s_nr[w].of(sc, t)
            done.mark(t, sc.activation(zs(ring, t), zs(ring, t), ACT.Identity, scale=rstd[w][0:r, k:k + 1],
                                       bias=nmr[w][0:r, k:k + 1]))

        return [(lag + i, f) for i, f in enumerate((bn, ag, root, rec, neg, norm))]

    def free(ring, t):
        if t >= ring:
            s_st[t % ring].of(v, t - ring)

    def store(ring, dst):
        def f(t):
            s_nm.of(sp, t)
            s_st[t % ring].mark(t, sp.dma_start(dst[cols(t), :], zs(ring, t)), 16)
        return f

    def transpose(src, given):
        def f(t):
            given.of(pe, t)
            if t >= 2:
                s_tc.of(pe, t - 2)
            x, r = src(t), rows(t)
            for h in range(2):
                ins = pe.transpose(PS[4 + t % 2][:, 128 * h:128 * h + r], x[:, 128 * h:128 * h + 128], ident[0:r, 0:r])
            s_tp.mark(t, ins)
        return f

    def turned(dst, scale=1.0):
        def f(t):
            s_tp.of(sc, t)
            p = PS[4 + t % 2][:, 0:256].rearrange("p (h w) -> p h w", h=2)[:, :, 0:rows(t)]
            s_tc.mark(t, sc.activation(dst[:, :, cols(t)], p, ACT.Identity, scale=scale))
        return f

    def stored(engine):
        for s in s_st + s_ts:
            s.by(engine)

    def table_rows(lag, table, width, lhs, rhs, ready):
        def mm(t):
            ready(t)
            if t >= 2:
                s_hs.of(pe, t - 2)
            for i in range(len(rhs)):
                ins = pe.matmul(PS[6 + t % 2][0:rows(t), 0:width], lhs(i, t), rhs[i], start=i == 0, stop=i == len(rhs) - 1)
            s_h.mark(t, ins)

        def scale(t):
            r = rows(t)
            s_h.of(sc, t)
            if t >= 4:
                s_ts[t % 4].of(sc, t - 4)
            s_hs.mark(t, sc.activation(XS[0:r, t % 4, 0:width], PS[6 + t % 2][0:r, 0:width], ACT.Identity, scale=dnm[0:r, t:t + 1]))

        def put(t):
            s_hs.of(sp, t)
            s_ts[t % 4].mark(t, sp.dma_start(table[cols(t), :], XS[0:rows(t), t % 4, 0:width]), 16)

        return [(lag, mm), (lag + 1, scale), (lag + 2, put)]

    def first_sums(width, lhs, rhs, init):
        for b in range(13):
            lo, n = 512 * b, min(512, N - 512 * b)
            if b >= 2:
                s_hc.of(pe, b - 2)
            for i in range(len(lhs)):
                ins = pe.matmul(PS[b % 2][0:width, 0:n], lhs[i], rhs(i, lo, n), start=i == 0, stop=i == len(lhs) - 1)
            s_hb.mark(b, ins)
            s_hb.of(v, b)
            s_hc.mark(b, v.tensor_tensor(init[:, lo:lo + n], PS[b % 2][0:width, 0:n], degB[0:width, lo:lo + n], ALU.mult))
        s_hc.by(v)

    def batch_norm(x, F, vec):
        B = 500
        nb = (N + B - 1) // B

        def stats(b):
            s_bb.of(v, b)
            for i in range(2 * b, min(2 * b + 2, 25)):
                ins = v.bn_stats(bst[0:F, i, :], x[:, 250 * i:250 * i + 250])
            s_bq.mark(b, ins)

        s_agg.by(sc)
        for b in range(nb):
            lo, n = B * b, min(B, N - B * b)
            s_bm.mark(b, v.tensor_tensor(x[:, lo:lo + n], x[:, lo:lo + n], degB[0:F, lo:lo + n], ALU.mult))
            s_bm.of(sc, b)
            s_bb.mark(b, sc.activation(x[:, lo:lo + n], x[:, lo:lo + n], ACT.Identity, bias=vec[:, 0:1]))
            if b >= 2:
                stats(b - 2)
        stats(nb - 2)
        stats(nb - 1)
        s_bq.by(v)
        s_ba.on(v.bn_aggr(bmv[0:F, :], bst[0:F, :, :]))
        s_ba.by(sc)
        s_q.on(sc.activation(bsc[0:F, 0:1], bmv[0:F, 1:2], ACT.Sqrt, bias=epsc[0:F, 0:1]))
        s_q.by(v)
        link(v.reciprocal(bsc[0:F, 1:2], bsc[0:F, 0:1]))
        link(v.tensor_tensor(bsc[0:F, 2:3], bsc[0:F, 1:2], vec[:, 1:2], ALU.mult))
        link(v.scalar_tensor_tensor(bsc[0:F, 3:4], bmv[0:F, 0:1], -1.0, bsc[0:F, 2:3], ALU.mult, ALU.mult))
        link(v.tensor_tensor(bsc[0:F, 3:4], bsc[0:F, 3:4], vec[:, 2:3], ALU.add))
        s_d.by(sc)

    def rectify(x, F):
        def f(t):
            if t % 4 == 0:
                lo, n = 128 * t, min(512, N - 128 * t)
                s_rl.mark(t // 4, sc.activation(x[:, lo:lo + n], x[:, lo:lo + n], ACT.Relu, scale=bsc[0:F, 2:3], bias=bsc[0:F, 3:4]))
        return f

    x1T = accT[:, 0, 0:N]
    x2T = accT[0:64, 1, 0:N]

    def spread():
        link(v.tensor_copy(cur[:, :, :], dst0[:, :, :]))
        link(v.tensor_copy(base[:, :], base0[:, :]))
        s_d.by(sp)
        last2 = lambda g: (chunks(g) + 1) // 2
        pairs = lambda g: 2 * g
        with nc.Fori(0, R, engines=LOOP0):
            def load_x(g):
                if g % LOADREGS == 0:
                    spread.los = nc.values_load_multi_w_load_instructions(
                        base[0:1, g:g + LOADREGS], engines=[ET.SP], min_val=0, max_val=LAST,
                        skip_runtime_bounds_check_because="held under LAST")[1]
                if g >= 4:
                    sp.wait_ge(s_Y, 2 * (g - 3))
                sp.dma_start(XR[:, g % 4, :], a["xpad"][bass.ds(spread.los[g % LOADREGS], 128), :]).then_inc(s_x[g % 4], 16)

            def source_rows(g):
                if g >= 2:
                    pe.wait_ge(s_b, g - 1)
                for j in range(chunks(g)):
                    c = CG * g + j
                    o = PS[g % 2][:, 128 * j:128 * j + 128]
                    pe.matmul(o, srch[:, c:c + 1].broadcast_to([128, 128]), identb[:, :], start=True, stop=False)
                    last = pe.matmul(o, srcl[:, c:c + 1].broadcast_to([128, 128]), identb[:, :], start=False, stop=True)
                last.then_inc(s_sr, 1)

            def prepare(g):
                k = chunks(g)
                if g >= 2:
                    v.wait_ge(s_M, g - 1)
                for j in range(k):
                    c = CG * g + j
                    v.tensor_scalar(Su[:, g % 2, j, :], iota[:, :], cur[:, g, j:j + 1], None, ALU.is_equal)
                    v.tensor_scalar(S[:, g % 2, j, :], iota[:, :], cur[:, g, j:j + 1], wgt[:, c:c + 1],
                                    ALU.is_equal, ALU.mult)
                v.wait_ge(s_sr, g + 1)
                v.tensor_tensor(Eq[:, g % 2, 0:k, :], PS[g % 2][:, 0:128 * k].rearrange("p (j e) -> p j e", j=k),
                                srcf[:, g, 0:k].unsqueeze(2).broadcast_to([128, k, 128]), ALU.is_equal).then_inc(s_eq, 1)
                v.wait_ge(s_eq, g + 1)
                for j in range(k):
                    last = v.tensor_tensor_reduce(out=junk[:, j, :], in0=Eq[:, g % 2, j, :], in1=lower[:, :], scale=1.0, scalar=0.0,
                                                  op0=ALU.mult, op1=ALU.add, accum_out=cnt[:, g, j:j + 1])
                last.then_inc(s_cn, 1)
                v.wait_ge(s_cn, 2 * g + 1)
                v.scalar_tensor_tensor(cnt[:, g, 0:k], cnt[:, g, 0:k], 0.0, spare[:, g, 0:k], ALU.is_gt, ALU.mult).then_inc(s_cn, 1)
                v.wait_ge(s_cn, 2 * g + 2)
                v.tensor_tensor(tgt[:, CG * g:CG * g + k], cnt[:, g, 0:k], srcA[:, g, 0:k], ALU.add).then_inc(s_b, 1)

            def routes(g):
                k = chunks(g)
                pe.wait_ge(s_b, g + 1)
                if g >= 2:
                    pe.wait_ge(s_da, g - 1)
                for j in range(k):
                    pe.matmul(PS[6 + g % 2][:, 0:W], onesb[:, :], Su[:, g % 2, j, :], start=j == 0, stop=j == k - 1)
                if g >= 2:
                    pe.wait_ge(s_mc, g - 1)
                for j in range(k):
                    last = pe.matmul(PS[2 + g % 2][:, 128 * j:128 * j + 128], S[:, g % 2, j, :], Eq[:, g % 2, j, :],
                                     start=True, stop=True)
                last.then_inc(s_M, 1)

            def routes_out(g):
                k = chunks(g)
                sc.wait_ge(s_M, g + 1)
                if g >= 2:
                    sc.wait_ge(s_Y, 2 * (g - 1))
                sc.activation(Ms[:, g % 2, 0:128 * k], PS[2 + g % 2][:, 0:128 * k], ACT.Identity).then_inc(s_mc, 1)

            def messages(g):
                pe.wait_ge(s_mc, g + 1)
                pe.wait_ge(s_x[g % 4], 16 * (g // 4 + 1))
                for q in range(2):
                    n = 2 * g + q
                    if n >= 2:
                        pe.wait_ge(s_yc, n - 1)
                    js = [j for j in (2 * q, 2 * q + 1) if j < chunks(g)]
                    for j in js:
                        last = pe.matmul(PS[4 + n % 2][:, D * (j % 2):D * (j % 2) + D], Ms[:, g % 2, 128 * j:128 * j + 128],
                                         XR[:, g % 4, :], start=True, stop=True)
                    if js:
                        last.then_inc(s_Y, 1)

            def messages_out(g):
                if g >= RING:
                    for j in range(CG):
                        if taken(j, g - RING):
                            sc.wait_ge(s_k[j], 16 * taken(j, g - RING))
                for q in range(2):
                    n = 2 * g + q
                    js = [j for j in (2 * q, 2 * q + 1) if j < chunks(g)]
                    if js:
                        sc.wait_ge(s_Y, n + 1)
                        sc.activation(G[:, g % RING, js[0]:js[-1] + 1, :],
                                      PS[4 + n % 2][:, 0:D * len(js)].rearrange("p (j d) -> p j d", j=len(js)),
                                      ACT.Identity).then_inc(s_yc, 1)

            for g in range(NG):
                load_x(g)
            source_rows(0)
            for g in range(NG + 1):
                if g + 1 < NG:
                    source_rows(g + 1)
                if g < NG:
                    routes(g)
                    routes_out(g)
                if g >= 1:
                    messages(g - 1)
                    messages_out(g - 1)
            uses = [0] * CG
            for g in range(NG):
                pool.wait_ge(s_b, g + 1)
                for j in range(chunks(g)):
                    c = CG * g + j
                    if j % 2 == 0:
                        pool.wait_ge(s_yc, 2 * g + j // 2 + 1)
                    n = copy_of(c)
                    if uses[n]:
                        pool.wait_ge(s_k[n], 16 * uses[n])
                    else:
                        s_zero[n].by(pool)
                    uses[n] += 1
                    pool.indirect_dma_start(A, bass.IndirectOffsetOnAxis(tgt[:, c:c + 1], 0), G[:, g % RING, j, :], None,
                                            compute_op=ALU.add).then_inc(s_k[n], 16)
            prepare(0)
            for g in range(NG):
                if g % LOADREGS == 0:
                    los = nc.values_load_multi_w_load_instructions(
                        base[0:1, g:g + LOADREGS], engines=[ET.DVE], min_val=0, max_val=LAST,
                        skip_runtime_bounds_check_because="held under LAST")[1]
                if g + 1 < NG:
                    prepare(g + 1)
                v.wait_ge(s_M, g + 1)
                if g:
                    v.wait_ge(s_da, g)
                dw = degB[:, bass.ds(los[g % LOADREGS], W)]
                v.tensor_tensor(dw, PS[6 + g % 2][:, 0:W], dw, ALU.add).then_inc(s_da, 1)

            for j in range(CG):
                pool.wait_ge(s_k[j], 16 * taken(j, NG - 1))
            for e, s in ((pool, s_end[0]), (pe, s_end[1]), (sc, s_end[2]), (sp, s_end[3])):
                e.sem_inc(s, 1)
                v.wait_ge(s, 1)
            v.wait_ge(s_da, NG)
            for s in s_x + s_end + [s_sr, s_b, s_eq, s_cn, s_M, s_mc, s_Y, s_yc, s_da]:
                v.sem_clear(s)
            v.tensor_scalar(cur[:, :, :], cur[:, :, :], float(W), None, ALU.subtract).then_inc(s_da, 1)
            v.tensor_scalar(base[:, :], base[:, :], float(W), float(LAST), ALU.add, ALU.min).then_inc(s_da, 1)
            v.wait_ge(s_da, 2)
            v.sem_clear(s_da)
            for i, e in ((0, pool), (1, pe), (3, sp)):
                v.sem_inc(s_go[i], 1)
                e.wait_ge(s_go[i], 1)
                e.sem_clear(s_go[i])
            pool.dma_reset(range(s_k[0].num, s_k[0].num + CG))
            for s in s_k:
                pool.sem_clear(s)
            pool.sem_inc(s_go[2], 1)
            sc.wait_ge(s_go[2], 1)
            sc.sem_clear(s_go[2])
        v.sem_inc(s_agg.sem, 1)
        s_agg.n += 1
        pool.sem_inc(s_spread.sem, 1)
        s_spread.n += 1

    s_x = [nc.alloc_semaphore(f"s_x{i}") for i in range(4)]
    s_k = [nc.alloc_semaphore(f"s_k{i}") for i in range(CG)]
    s_end = [nc.alloc_semaphore(f"s_end{i}") for i in range(4)]
    s_go = [nc.alloc_semaphore(f"s_go{i}") for i in range(4)]
    s_sr, s_b, s_eq, s_cn, s_M, s_mc, s_Y, s_yc, s_da = (
        nc.alloc_semaphore(n) for n in ("s_sr", "s_b", "s_eq", "s_cn", "s_M", "s_mc", "s_Y", "s_yc", "s_da"))
    s_spread = count("s_spread")
    Eq = Z[:, 0:4, :].rearrange("p a b -> p (a b)").rearrange("p (r j e) -> p r j e", r=2, j=CG)
    Ms = Z[:, 4:8, :].rearrange("p a b -> p (a b)").rearrange("p (r n) -> p r n", r=2)
    junk = Z[:, 8:10, :].rearrange("p a b -> p (a b)").rearrange("p (j e) -> p j e", j=CG)

    spread()
    s_agg.by(sc)
    s_spread.by(sp)
    s_agg.by(pe)
    s_agg.by(v)
    link(v.memset(dnm[:, :], 0.0))
    s_d.by(sc)
    s_dq, s_dr, s_nq = names("dq", "dr", "nq")

    def load_sums(t):
        r, slot = rows(t), t % RING
        if t >= RING:
            s_ta.of(sp, t - RING)
        s_al[slot].mark(t, sp.dma_start(G[0:r, slot, :, :], A.rearrange("(k n) d -> n k d", k=CG)[cols(t), :, :]), 16)

    def add_pairs(t):
        r, slot = rows(t), t % RING
        s_al[slot].of(pool, t)
        s_a1.mark(t, pool.tensor_tensor(G[0:r, slot, 0:2, :], G[0:r, slot, 0:2, :], G[0:r, slot, 2:4, :], ALU.add))

    def add_last(t):
        r, slot = rows(t), t % RING
        s_a1.of(v, t)
        s_a2.mark(t, v.tensor_tensor(G[0:r, slot, 0, :], G[0:r, slot, 0, :], G[0:r, slot, 1, :], ALU.add))

    def turn_sums(t):
        r, slot = rows(t), t % RING
        s_a2.of(pe, t)
        if t >= 2:
            s_ca.of(pe, t - 2)
        for h in range(2):
            pe.transpose(PS[t % 2][:, 128 * h:128 * h + r], G[0:r, slot, 0, 128 * h:128 * h + 128], ident[0:r, 0:r])
        s_ta.mark(t, pe.matmul(PS[t % 2][0:r, 256:257], degB[0:1, cols(t)], ones[0:1, 0:1], start=True, stop=True))

    def sums_out(t):
        s_ta.of(sc, t)
        p = PS[t % 2][:, 0:256].rearrange("p (h w) -> p h w", h=2)[:, :, 0:rows(t)]
        s_nq.mark(t, sc.activation(dnm[0:rows(t), t:t + 1], PS[t % 2][0:rows(t), 256:257], ACT.Sqrt))
        s_ca.mark(t, sc.activation(accT[:, :, cols(t)], p, ACT.Identity))

    def degree_roots(t):
        s_ta.of(sc, t)
        s_dq.mark(t, sc.activation(degB[:, cols(t)], degB[:, cols(t)], ACT.Sqrt))

    def degree_inverses(t):
        s_nq.of(v, t)
        v.reciprocal(dnm[0:rows(t), t:t + 1], dnm[0:rows(t), t:t + 1])
        s_dq.of(v, t)
        s_dr.mark(t, v.reciprocal(degB[:, cols(t)], degB[:, cols(t)]))

    def add_residual(ring):
        def f(t):
            free(ring, t)
            s_ld[t % 4].of(v, t)
            s_mm.of(v, t)
            s_z.mark(t, v.tensor_tensor(zs(ring, t), PS[2 + t % 2][0:rows(t), 0:D], XR[0:rows(t), t % 4, :], ALU.add))
        return f

    pipeline([(0, load_sums), (2, add_pairs), (3, add_last), (4, turn_sums), (5, sums_out), (5, degree_roots), (6, degree_inverses), (4, residual(a["xpad"])),
              (6, multiply(lambda t: [(accT[:, h, cols(t)], W0[:, h, :]) for h in range(2)], lambda t: s_ca.of(pe, t))),
              (7, add_residual(ZR0))]
             + normalise(8, ZR0, 0, s_z, s_nm)
             + [(14, store(ZR0, X1)), (14, transpose(lambda t: zs(ZR0, t), s_nm)), (15, turned(xT))]
             + table_rows(16, T1, 128, lambda i, t: xT[:, i, cols(t)], [W1[:, 0, :], W1[:, 1, :]], lambda t: (s_tc.of(pe, t), s_dr.of(sc, t))))

    s_dr.by(sc)
    for s in s_ts:
        s.by(pool)
    s_ta.by(pool)
    s_mm.by(v)
    s_ca.by(pe)
    first_sums(128, [W1[:, 0, :], W1[:, 1, :]], lambda i, lo, n: xT[:, i, lo:lo + n], x1T)
    aggregate(T1, 128, lambda lo: accT[:, 0, bass.ds(lo, W)], False)
    batch_norm(x1T, 128, vec1)
    pipeline([(0, rectify(x1T, 128))]
             + table_rows(1, T2, 64, lambda i, t: accT[:, 0, cols(t)], [W2[:, :]], lambda t: s_rl.of(pe, t // 4)))
    for s in s_ts:
        s.by(pool)
    first_sums(64, [W2[:, :]], lambda i, lo, n: accT[:, 0, lo:lo + n], x2T)
    aggregate(T2, 64, lambda lo: accT[0:64, 1, bass.ds(lo, W)], False)
    stored(sp)
    batch_norm(x2T, 64, vec2)
    s_e.on(v.tensor_scalar(e1[:, :], e1[:, :], 1.0, None, ALU.add))
    s_e.by(sc)
    s_e.by(pe)

    def add_bias(t):
        free(ZR, t)
        s_mm.of(v, t)
        s_pb.mark(t, v.tensor_tensor(zs(ZR, t), PS[2 + t % 2][0:rows(t), 0:D], rowb[0:rows(t), 0, :], ALU.add))

    def relu_residual(t):
        s_pb.of(v, t)
        s_ld[t % 4].of(v, t)
        s_z.mark(t, v.scalar_tensor_tensor(zs(ZR, t), zs(ZR, t), 0.0, XR[0:rows(t), t % 4, :], ALU.max, ALU.add))

    def cat(t):
        return [(xT[:, 0, cols(t)], Wf[:, 0, :]), (xT[:, 1, cols(t)], Wf[:, 1, :]), (accT[:, 0, cols(t)], Wf[:, 2, :]),
                (accT[0:64, 1, cols(t)], Wf3[:, :])]

    pipeline([(0, rectify(x2T, 64)), (0, residual(X1)), (1, multiply(cat, lambda t: s_rl.of(pe, t // 4))), (2, add_bias),
              (3, relu_residual)]
             + normalise(4, ZR, 0, s_z, s_nm)
             + [(10, store(ZR, X2)), (10, transpose(lambda t: zs(ZR, t), s_nm)), (11, turned(accT, e1[:, 0:1]))])

    stored(pool)
    s_tp.by(pool)
    s_tc.by(v)
    aggregate(X2, D, wide, True)
    stored(sp)
    s_agg.by(pe)

    def hidden(t):
        if t % 4:
            return
        lo, n = 128 * t, min(512, N - 128 * t)
        for o in range(2):
            i = t // 2 + o
            if i >= 2:
                s_uc.of(pe, i - 2)
            for h in range(2):
                ins = pe.matmul(PS[i % 2][:, 0:n], M1[:, h, 128 * o:128 * o + 128], accT[:, h, lo:lo + n], start=h == 0, stop=h == 1)
            s_u.mark(i, ins)

    def hidden_out(t):
        if t % 4:
            return
        lo, n = 128 * t, min(512, N - 128 * t)
        for o in range(2):
            i = t // 2 + o
            s_u.of(sc, i)
            s_uc.mark(i, sc.activation(xT[:, o, lo:lo + n], PS[i % 2][:, 0:n], ACT.Relu, bias=mb1[:, o:o + 1]))

    def bias_residual(t):
        r = rows(t)
        s_ld[t % 4].of(pool, t)
        s_pb.mark(t, pool.tensor_tensor(XR[0:r, t % 4, :], XR[0:r, t % 4, :], rowb[0:r, 1, :], ALU.add))

    def add_biased(t):
        free(ZR, t)
        s_pb.of(v, t)
        s_mm.of(v, t)
        s_z.mark(t, v.tensor_tensor(zs(ZR, t), PS[2 + t % 2][0:rows(t), 0:D], XR[0:rows(t), t % 4, :], ALU.add))

    def by_degree(t):
        r = rows(t)
        s_nm.of(v, t)
        if t >= 4:
            s_ts[t % 4].of(v, t - 4)
            s_tp.of(v, t - 4)
        s_xs.mark(t, v.tensor_scalar(XS[0:r, t % 4, :], zs(ZR, t), dnm[0:r, t:t + 1], None, ALU.mult))

    def put_table(t):
        s_xs.of(sp, t)
        s_ts[t % 4].mark(t, sp.dma_start(T3[cols(t), :], XS[0:rows(t), t % 4, :]), 16)

    pipeline([(0, hidden), (1, hidden_out), (1, residual(X2)), (3, bias_residual),
              (4, multiply(lambda t: [(xT[:, h, cols(t)], M2[:, h, :]) for h in range(2)], lambda t: s_uc.of(pe, 2 * (t // 4) + 1))),
              (5, add_biased)]
             + normalise(6, ZR, 0, s_z, s_nm)
             + [(12, store(ZR, X3)), (12, by_degree), (13, put_table), (13, transpose(lambda t: XS[0:rows(t), t % 4, :], s_xs)),
                (14, turned(accT))])

    stored(pool)
    s_xs.by(pool)
    s_tc.by(v)
    aggregate(T3, D, wide, False)
    stored(sp)
    s_agg.by(pe)

    def convolved(t):
        r = rows(t)
        free(ZR, t)
        s_mm.of(v, t)
        s_a1.mark(t, v.scalar_tensor_tensor(zs(ZR, t), PS[2 + t % 2][0:r, 0:D], dnm[0:r, t:t + 1], l3[0:r, 0, :], ALU.mult, ALU.add))

    def gamma(t):
        s_n1.of(pool, t)
        s_ga.mark(t, pool.tensor_tensor(zs(ZR, t), zs(ZR, t), l3[0:rows(t), 1, :], ALU.mult))

    def beta(t):
        s_ga.of(pool, t)
        s_be.mark(t, pool.tensor_tensor(zs(ZR, t), zs(ZR, t), l3[0:rows(t), 2, :], ALU.add))

    def relu_residual3(t):
        s_be.of(v, t)
        s_ld[t % 4].of(v, t)
        s_z.mark(t, v.scalar_tensor_tensor(zs(ZR, t), zs(ZR, t), 0.0, XR[0:rows(t), t % 4, :], ALU.max, ALU.add))

    def multiply3(t):
        if t >= 2:
            s_a1.of(pe, t - 2)
        for h in range(2):
            ins = pe.matmul(PS[2 + t % 2][0:rows(t), 0:D], accT[:, h, cols(t)], W3[:, h, :], start=h == 0, stop=h == 1)
        s_mm.mark(t, ins)

    pipeline([(0, multiply3), (1, convolved)] + normalise(2, ZR, 1, s_a1, s_n1)
             + [(9, gamma), (10, beta), (8, residual(X3)), (11, relu_residual3)]
             + normalise(12, ZR, 0, s_z, s_nm) + [(18, store(ZR, out))])
    stored(sp)


_GIVEN = ["xpad", "src", "dst", "edge_weight", "L0_gnn_W", "L1_gnn_W1", "L1_gnn_W2", "L1_gnn_Wfc", "L1_gnn_bfc", "L2_gnn_eps",
          "L2_gnn_w1", "L2_gnn_b1", "L2_gnn_w2", "L2_gnn_b2", "L3_gnn_W", "L3_gnn_b", "L3_gnn_gamma", "L3_gnn_beta",
          "vec1", "vec2"]


def kernel(**inputs):
    import numpy as np
    import concourse.bacc as bacc
    from concourse.bass_utils import run_bass_kernel_spmd

    given = {k: np.asarray(v) for k, v in inputs.items()}

    def by_chunk(x, n, fill):
        full = np.full(128 * n, fill, x.dtype)
        full[:E] = x
        return full.reshape(n, 128).T

    given["src"] = by_chunk(given["src"], NC, 0)
    given["dst"] = by_chunk(given["dst"], NG * CG, -1)
    given["edge_weight"] = by_chunk(given["edge_weight"], NG * CG, 0)
    given["L0_gnn_W"] = given["L0_gnn_W"].T
    given["xpad"] = np.concatenate([given["x"], np.zeros((AW - N, D), given["x"].dtype)])
    given["L3_gnn_W"] = given["L3_gnn_W"].T
    for k in ("L3_gnn_b", "L3_gnn_gamma", "L3_gnn_beta", "L1_gnn_bfc", "L2_gnn_b2"):
        given[k] = np.broadcast_to(given[k], (128, D))
    given["L2_gnn_eps"] = np.broadcast_to(given["L2_gnn_eps"].reshape(1, 1), (128, 1))
    given["L2_gnn_b1"] = given["L2_gnn_b1"].reshape(2, 128).T
    given["vec1"] = np.stack([given["L1_gnn_b1"], given["L1_gnn_g1"], given["L1_gnn_be1"]], axis=1)
    given["vec2"] = np.stack([given["L1_gnn_b2"], given["L1_gnn_g2"], given["L1_gnn_be2"]], axis=1)

    nc = bacc.Bacc("TRN2", target_bir_lowering=False, num_devices=1)
    arrays, args = {}, {}
    for name in _GIVEN:
        x = np.ascontiguousarray(given[name])
        arrays[f"in_{name}"] = x
        args[name] = nc.dram_tensor(f"in_{name}", x.shape, mybir.dt.from_np(x.dtype), kind="ExternalInput").ap()
    out = nc.dram_tensor("out_y", (N, D), F32, kind="ExternalOutput").ap()
    build(nc, args, out)
    r = run_bass_kernel_spmd(nc, [arrays], core_ids=[0])
    return r.results[0]["out_y"]
```
